# Optimizing a Trainium2 kernel written in Bass

```python
import numpy as np
import jax
import jax.numpy as jnp

def _softmax(x, axis=-1):
    return jax.nn.softmax(x, axis=axis)

def _gelu(x):
    return jax.nn.gelu(x, approximate=True)

def _silu(x):
    return jax.nn.silu(x)

def _sigmoid(x):
    return jax.nn.sigmoid(x)

def _layernorm(x, axis=-1, eps=1e-05):
    m = jnp.mean(x, axis=axis, keepdims=True)
    v = jnp.var(x, axis=axis, keepdims=True)
    return (x - m) / jnp.sqrt(v + eps)

def _scatter_add(tgt, idx, src, axis=0):
    return tgt.at[idx].add(src)

def _segment_sum(src, seg, n):
    return jax.ops.segment_sum(src, seg, n)
kernel_name = 'mk_decoder_postln_d1_seqx_r8_bb6aeb'

def setup_inputs(seed: int=0):
    np.random.seed(seed)
    _w = jnp.asarray

    def _rec_inputs():
        import jax
        import jax.numpy as jnp
        _rk = jax.random.key(seed)
        x = -0.0003929 + 0.9999 * jax.random.normal(jax.random.fold_in(_rk, 1), (2, 256, 512), jnp.float32)
        _lenS = 256 - jax.random.randint(jax.random.fold_in(_rk, 7), (2,), 0, max(1, 256 // 4) + 1, jnp.int32)
        _lenS2 = 512 - jax.random.randint(jax.random.fold_in(_rk, 8), (2,), 0, max(1, 512 // 4) + 1, jnp.int32)
        _ctx_1024P = jax.random.normal(jax.random.fold_in(_rk, 11), (2, 16, 128), jnp.float32)
        _ctx_1024c = jax.random.dirichlet(jax.random.fold_in(_rk, 511), 0.3 * jnp.ones((16,), jnp.float32), (2, 512))
        _ctx_1024t = jnp.einsum('bsk,bkd->bsd', _ctx_1024c, _ctx_1024P)
        _ctx_1024t = _ctx_1024t * jax.lax.rsqrt(jnp.mean(jnp.square(_ctx_1024t)) + 1e-12) * 0.953939
        ctx_1024 = -1.39393e-06 + 0.999914 * (_ctx_1024t + 0.3 * jax.random.normal(jax.random.fold_in(_rk, 611), (2, 512, 128), jnp.float32))
        _validS = jnp.arange(256)[None, :] < _lenS[:, None]
        _validS2 = jnp.arange(512)[None, :] < _lenS2[:, None]
        _causal = jnp.tril(jnp.ones((256, 256), dtype=bool))
        mask_SxS2_ff0 = jnp.where(jnp.ones((256, 512), dtype=bool), 0.0, -1000000000.0).astype(jnp.float32)
        return (x, ctx_1024, mask_SxS2_ff0)
    x, ctx_1024, mask_SxS2_ff0 = _rec_inputs()

    def _L0_attn_setup():
        import jax, jax.numpy as jnp
        import numpy as np
        HIDDEN = 512
        N_HEADS = 32
        N_KV_HEADS = 8
        HEAD_DIM = HIDDEN // N_HEADS
        N_REP = N_HEADS // N_KV_HEADS
        KV_DIM = N_KV_HEADS * HEAD_DIM

        def _kaiming_uniform(key, out_f, in_f):
            bound = 1.0 / np.sqrt(in_f)
            return jax.random.uniform(key, (out_f, in_f), jnp.float32, -bound, bound)

        def bitnet_linear(x, weight, scale_param):
            s = jnp.maximum(jnp.mean(jnp.abs(weight), axis=1), 1e-08)
            binary_w = jnp.sign(weight / s[:, None])
            y = jnp.einsum('bsi,oi->bso', x, binary_w)
            y = y * (s * scale_param)[None, None, :]
            return jnp.nan_to_num(y, nan=0.0, posinf=1000000.0, neginf=-1000000.0)
        key = jax.random.key(seed)
        ks = jax.random.split(key, 5)
        return {'hidden_states': jax.random.normal(ks[0], (1, 256, HIDDEN), jnp.float32), 'q_weight': _kaiming_uniform(ks[1], HIDDEN, HIDDEN), 'q_scale': jnp.ones((HIDDEN,), jnp.float32), 'k_weight': _kaiming_uniform(ks[2], KV_DIM, HIDDEN), 'k_scale': jnp.ones((KV_DIM,), jnp.float32), 'v_weight': _kaiming_uniform(ks[3], KV_DIM, HIDDEN), 'v_scale': jnp.ones((KV_DIM,), jnp.float32), 'o_weight': _kaiming_uniform(ks[4], HIDDEN, HIDDEN), 'o_scale': jnp.ones((HIDDEN,), jnp.float32)}
    _L0_attn_all = _L0_attn_setup()
    _L0_attn_in = {k: v for k, v in _L0_attn_all.items() if k in ('q_weight', 'q_scale', 'k_weight', 'k_scale', 'v_weight', 'v_scale', 'o_weight', 'o_scale')}
    del _L0_attn_all

    def _L0_xattn_setup():
        import math
        import jax, jax.numpy as jnp
        import numpy as np
        N_HEADS = 32
        N_KV_HEADS = 8
        N_REP = N_HEADS // N_KV_HEADS
        HEAD_DIM = 512 // N_HEADS
        key = jax.random.key(seed)
        kq, kk, kv = jax.random.split(key, 3)
        B, S, T = (2, 256, 256)
        q = jax.random.normal(kq, (B, S, N_HEADS * HEAD_DIM), dtype=jnp.float32)
        k = jax.random.normal(kk, (B, T, N_KV_HEADS * HEAD_DIM), dtype=jnp.float32)
        v = jax.random.normal(kv, (B, T, N_KV_HEADS * HEAD_DIM), dtype=jnp.float32)
        mask = jnp.zeros((S, T), dtype=jnp.float32)
        return {'q': q, 'k': k, 'v': v, 'start_pos': 0, 'mask': mask}
    _L0_xattn_all = _L0_xattn_setup()
    _L0_xattn_in = {k: v for k, v in _L0_xattn_all.items() if k in ()}
    del _L0_xattn_all

    def _L0_ffn_setup():
        import jax, jax.numpy as jnp
        import numpy as np
        B_L, B_H = (4, 8)
        LIN_SLOPE, LIN_INTER, EST_T = (1.0, 0.0, 64.0)
        BATCH, SEQ, IN_F, OUT_F = (4, 256, 512, 512)
        MAX_BITS = 8

        def dequant_kbit(qweight, lut, bit):
            O, I32 = (qweight.shape[1], qweight.shape[2])
            shifts = jnp.arange(32, dtype=jnp.int32)
            idx = jnp.zeros((O, I32 * 32), dtype=jnp.int32)
            for p in range(bit):
                bits = (qweight[p][:, :, None] >> shifts & 1).reshape(O, I32 * 32)
                idx = idx | bits << p
            return jnp.take_along_axis(lut, idx, axis=1)
        key = jax.random.key(seed)
        k = jax.random.split(key, 5)
        x = jax.random.normal(k[0], (BATCH, SEQ, IN_F), dtype=jnp.float32)
        qweight = jax.random.randint(k[1], (MAX_BITS, OUT_F, IN_F // 32), 0, 2147483647, dtype=jnp.int32)
        lut4 = jax.random.normal(k[2], (OUT_F, 2 ** B_L), dtype=jnp.float32) * 0.02
        lut8 = jax.random.normal(k[3], (OUT_F, 2 ** B_H), dtype=jnp.float32) * 0.02
        bias = jax.random.normal(k[4], (OUT_F,), dtype=jnp.float32) * 0.01
        return {'x': x, 'qweight': qweight, 'lut4': lut4, 'lut8': lut8, 'bias': bias}
    _L0_ffn_all = _L0_ffn_setup()
    _L0_ffn_in = {k: v for k, v in _L0_ffn_all.items() if k in ('qweight', 'lut4', 'lut8', 'bias')}
    del _L0_ffn_all
    return {'x': x, 'ctx_1024': ctx_1024, 'mask_SxS2_ff0': mask_SxS2_ff0, 'L0_attn_q_weight': _L0_attn_in['q_weight'], 'L0_attn_q_scale': _L0_attn_in['q_scale'], 'L0_attn_k_weight': _L0_attn_in['k_weight'], 'L0_attn_k_scale': _L0_attn_in['k_scale'], 'L0_attn_v_weight': _L0_attn_in['v_weight'], 'L0_attn_v_scale': _L0_attn_in['v_scale'], 'L0_attn_o_weight': _L0_attn_in['o_weight'], 'L0_attn_o_scale': _L0_attn_in['o_scale'], 'L0_ffn_qweight': _L0_ffn_in['qweight'], 'L0_ffn_lut4': _L0_ffn_in['lut4'], 'L0_ffn_lut8': _L0_ffn_in['lut8'], 'L0_ffn_bias': _L0_ffn_in['bias']}

def reference(x, ctx_1024, mask_SxS2_ff0, L0_attn_q_weight, L0_attn_q_scale, L0_attn_k_weight, L0_attn_k_scale, L0_attn_v_weight, L0_attn_v_scale, L0_attn_o_weight, L0_attn_o_scale, L0_ffn_qweight, L0_ffn_lut4, L0_ffn_lut8, L0_ffn_bias):
    import jax
    import jax.numpy as jnp

    def _L0_attn_ref(hidden_states, q_weight, q_scale, k_weight, k_scale, v_weight, v_scale, o_weight, o_scale):
        import jax, jax.numpy as jnp
        import numpy as np
        HIDDEN = 512
        N_HEADS = 32
        N_KV_HEADS = 8
        HEAD_DIM = HIDDEN // N_HEADS
        N_REP = N_HEADS // N_KV_HEADS
        KV_DIM = N_KV_HEADS * HEAD_DIM

        def _kaiming_uniform(key, out_f, in_f):
            bound = 1.0 / np.sqrt(in_f)
            return jax.random.uniform(key, (out_f, in_f), jnp.float32, -bound, bound)

        def bitnet_linear(x, weight, scale_param):
            s = jnp.maximum(jnp.mean(jnp.abs(weight), axis=1), 1e-08)
            binary_w = jnp.sign(weight / s[:, None])
            y = jnp.einsum('bsi,oi->bso', x, binary_w)
            y = y * (s * scale_param)[None, None, :]
            return jnp.nan_to_num(y, nan=0.0, posinf=1000000.0, neginf=-1000000.0)
        b, s, _ = hidden_states.shape
        q = bitnet_linear(hidden_states, q_weight, q_scale)
        k = bitnet_linear(hidden_states, k_weight, k_scale)
        v = bitnet_linear(hidden_states, v_weight, v_scale)
        q = q.reshape(b, s, N_HEADS, HEAD_DIM).transpose(0, 2, 1, 3)
        k = k.reshape(b, s, N_KV_HEADS, HEAD_DIM).transpose(0, 2, 1, 3)
        v = v.reshape(b, s, N_KV_HEADS, HEAD_DIM).transpose(0, 2, 1, 3)
        k = jnp.repeat(k, N_REP, axis=1)
        v = jnp.repeat(v, N_REP, axis=1)
        scores = jnp.einsum('bhqd,bhkd->bhqk', q, k) / np.sqrt(HEAD_DIM)
        attn = jax.nn.softmax(scores, axis=-1)
        out = jnp.einsum('bhqk,bhkd->bhqd', attn, v)
        out = out.transpose(0, 2, 1, 3).reshape(b, s, HIDDEN)
        return bitnet_linear(out, o_weight, o_scale)

    def _L0_xattn_ref(q, k, v, start_pos, mask):
        import math
        import jax, jax.numpy as jnp
        import numpy as np
        N_HEADS = 32
        N_KV_HEADS = 8
        N_REP = N_HEADS // N_KV_HEADS
        HEAD_DIM = 512 // N_HEADS
        b, s, _ = q.shape
        t = k.shape[1]
        xq = q.reshape(b, s, N_KV_HEADS, N_REP, HEAD_DIM)
        xk = k.reshape(b, t, N_KV_HEADS, HEAD_DIM)
        xv = v.reshape(b, t, N_KV_HEADS, HEAD_DIM)
        scores = jnp.einsum('bsgrd,btgd->bgrst', xq, xk) / math.sqrt(HEAD_DIM)
        scores = scores + mask
        probs = jax.nn.softmax(scores.astype(jnp.float32), axis=-1).astype(q.dtype)
        out = jnp.einsum('bgrst,btgd->bsgrd', probs, xv)
        return out.reshape(b, s, N_HEADS * HEAD_DIM)

    def _L0_ffn_ref(x, qweight, lut4, lut8, bias):
        import jax, jax.numpy as jnp
        import numpy as np
        B_L, B_H = (4, 8)
        LIN_SLOPE, LIN_INTER, EST_T = (1.0, 0.0, 64.0)
        BATCH, SEQ, IN_F, OUT_F = (4, 256, 512, 512)
        MAX_BITS = 8

        def dequant_kbit(qweight, lut, bit):
            O, I32 = (qweight.shape[1], qweight.shape[2])
            shifts = jnp.arange(32, dtype=jnp.int32)
            idx = jnp.zeros((O, I32 * 32), dtype=jnp.int32)
            for p in range(bit):
                bits = (qweight[p][:, :, None] >> shifts & 1).reshape(O, I32 * 32)
                idx = idx | bits << p
            return jnp.take_along_axis(lut, idx, axis=1)
        e = jnp.linalg.norm(x, axis=-1) * LIN_SLOPE + LIN_INTER
        mask = e > EST_T
        w_l = dequant_kbit(qweight, lut4, B_L)
        w_h = dequant_kbit(qweight, lut8, B_H)
        y_l = jnp.einsum('bsi,oi->bso', x, w_l)
        y_h = jnp.einsum('bsi,oi->bso', x, w_h)
        y = jnp.where(mask[..., None], y_h, y_l) + bias
        return y
    x = _layernorm(x + _L0_attn_ref(x, L0_attn_q_weight, L0_attn_q_scale, L0_attn_k_weight, L0_attn_k_scale, L0_attn_v_weight, L0_attn_v_scale, L0_attn_o_weight, L0_attn_o_scale), axis=-1)
    x = _layernorm(x + _L0_xattn_ref(x, ctx_1024, ctx_1024, 0, mask_SxS2_ff0), axis=-1)
    x = _layernorm(x + _L0_ffn_ref(x, L0_ffn_qweight, L0_ffn_lut4, L0_ffn_lut8, L0_ffn_bias), axis=-1)
    return x

_drawn_inputs = setup_inputs


def setup_inputs(seed=0):
    import zlib

    import numpy as np

    out = dict(_drawn_inputs(seed))
    spreads = {'mask_SxS2_ff0': (0.0, 0.8),
     'L0_attn_q_scale': (1.0, 0.6),
     'L0_attn_k_scale': (1.0, 0.6),
     'L0_attn_v_scale': (1.0, 0.6),
     'L0_attn_o_scale': (1.0, 0.6)}
    factors = {'L0_attn_q_weight': 8.0,
     'L0_attn_k_weight': 7.203,
     'L0_attn_v_weight': 3.505,
     'L0_attn_o_weight': 3.456,
     'L0_ffn_bias': 6.304}
    for name, (base, spread) in spreads.items():
        noise = np.random.default_rng([zlib.crc32(name.encode()), seed]).standard_normal(out[name].shape)
        drawn = base * np.exp(spread * noise) if base else spread * noise
        out[name] = jnp.asarray(drawn.astype(out[name].dtype))
    for name, factor in factors.items():
        out[name] = (out[name] * factor).astype(out[name].dtype)
    return out
```

```python
from contextlib import ExitStack

import concourse.bass as bass
from concourse import mybir

F32 = mybir.dt.float32
BF16 = mybir.dt.bfloat16
I32 = mybir.dt.int32
ALU = mybir.AluOpType
ACT = mybir.ActivationFunctionType
AX = mybir.AxisListType

P = 128
B, S, D = 2, 256, 512
T2 = 512
H, G, HD = 32, 8, 16
R = H // G
N = B * S
NT = N // P
DT = D // P
QT = S // P
KV = G * HD
VW = 32
Q_PART = (0, 0, 1, 1, 0, 2)
K_PART = (0, 1, 0, 1, 2, 0)
SLOTS = len(Q_PART)
KR = SLOTS * HD
EPS = 1e-5
LOWEST = -3.4e38
LUT = 16
PLANES = 4
BITS = 32
WORDS = D // BITS
NORM2 = 64.0 * 64.0

UNITS = 2 * B * G
SM_RING = 3
PT_RING = 3


def layer(u):
    return u // (B * G)


def batch(u):
    return u // G % B


def group(u):
    return u % G


def key_tiles(u):
    return (T2 if layer(u) else S) // P


def first_chunk(u):
    return sum(key_tiles(v) for v in range(u))


def fills(u):
    return R * QT if layer(u) else R


def first_fill(u):
    return sum(fills(v) for v in range(u))


def kernel_body(nc, x_tok, x_T, wq_T, wq, wkv_T, wkv, wo_T, wo, scales_in,
                ctx, ctx_T, mask, qweight, lut4, lut8, bias, out):
    SIDE = {u: [] for u in range(UNITS + 4)}
    for b in range(B):
        base = G * (b + 1)
        for t in range(b * QT, (b + 1) * QT):
            SIDE[base].append(("turn_o", t))
            SIDE[base + 1].append(("project_o", t))
            SIDE[base + 2].append(("turn_x1", t))
        base = B * G + G * (b + 1)
        for t in range(b * QT, (b + 1) * QT):
            SIDE[base].append(("norm_x2", t))
            SIDE[base + 1 if b == 0 else base].append(("turn_x2", t))
            SIDE[base + 2 if b == 0 else base].append(("ffn", t))
    for o in range(DT):
        SIDE[3 * G].append(("turn_w", o))
    uses = []
    for u in range(UNITS + 1):
        if u >= 1:
            uses.append(("turn_unit", u - 1))
        uses += [s for s in SIDE[u] if s[0] != "norm_x2"]
    PM_USE = {k: n for n, k in enumerate(uses)}
    assert len(PM_USE) == len(uses)

    with ExitStack() as stack:
        def sb(name, shape, dt=F32):
            return stack.enter_context(nc.sbuf_tensor(name, shape, dt))

        def sem(name):
            return stack.enter_context(nc.semaphore(name))

        ident = sb("ident", [P, P])
        ones = sb("ones", [P, P])
        xT = sb("xT", [P, DT, N])
        wqT = sb("wqT", [P, DT, D])
        wkvT = sb("wkvT", [P, DT, 2 * KV])
        woT = sb("woT", [P, DT, D])
        x = sb("x", [P, NT, D])
        O = sb("O", [P, NT, D])
        QA = sb("QA", [P, H, N], BF16)
        KA1 = sb("KA1", [P, G, N], BF16)
        KA2 = sb("KA2", [P, G, B * T2], BF16)
        V1 = sb("V1", [P, NT, G, VW])
        V2 = sb("V2", [P, B * T2 // P, G, VW])
        SM = sb("SM", [P, SM_RING, R * QT, T2])
        PTs = sb("PTs", [P, PT_RING, R * S])
        maskq = sb("maskq", [P, QT, T2])
        mx = sb("mx", [P, SM_RING, R * QT])
        OT = sb("OT", [P, S])
        rsum = sb("rsum", [P, QT, R, 1])
        idx = sb("idx", [P, DT, D], BF16)
        code = sb("code", [P, 2, DT, D], BF16)
        lut = sb("lut", [P, DT, LUT])
        planes = sb("planes", [P, DT, PLANES, WORDS], I32)
        scl = sb("scl", [P, 16])
        mean = sb("mean", [P, 16])
        sv = sb("sv", [P, KV])
        so = sb("so", [P, D])
        biasb = sb("biasb", [P, D])
        oT = sb("oT", [P, DT, P])
        xq = sb("xq", [P, DT, P])
        parts = sb("parts", [P, 3, DT, P], BF16)
        x2T = sb("x2T", [P, DT, P])
        tmp = sb("tmp", [P, D])
        stats = sb("stats", [P, 6])
        mv = sb("mv", [P, 2])
        rstd = sb("rstd", [P, 1])
        var = sb("var", [P, 1])
        half = sb("half", [P, 1])
        wq_n = SM[:, 0].rearrange("p a t -> p (a t)")[:, 0:DT * D].rearrange("p (o i) -> p o i", o=DT)
        wkv_n = SM[:, 0].rearrange("p a t -> p (a t)")[:, DT * D:DT * D + 2 * D].rearrange("p (o i) -> p o i", o=2)
        wo_n = SM[:, 1].rearrange("p a t -> p (a t)")[:, 0:DT * D].rearrange("p (o i) -> p o i", o=DT)
        cT = SM[:, 1].rearrange("p a t -> p (a t)")[:, DT * D:DT * D + B * T2]
        cN = SM[:, 1].rearrange("p a t -> p (a t)")[:, DT * D + B * T2:DT * D + 2 * B * T2]
        qf = SM[:, 2].rearrange("p a t -> p (a t)")[:, 0:DT * N].rearrange("p (o n) -> p o n", o=DT)
        kf = SM[:, 2].rearrange("p a t -> p (a t)")[:, DT * N:DT * N + N]
        diag = SM[:, 2].rearrange("p a t -> p (a t)")[:, (DT + 1) * N:(DT + 1) * (N + P)].rearrange("p (o n) -> p o n", o=DT + 1)
        pt_flat = PTs[:].rearrange("p a t -> p (a t)").bitcast(BF16)
        q_parts = pt_flat[:, 0:3 * DT * N].rearrange("p (s o n) -> p s o n", s=3, o=DT)
        k_parts = V2[:].rearrange("p a g v -> p (a g v)").bitcast(BF16)[:, 0:3 * N].rearrange("p (s n) -> p s n", s=3)
        c_parts = O[:].rearrange("p a d -> p (a d)").bitcast(BF16)[:, 0:3 * B * T2].rearrange("p (s n) -> p s n", s=3)
        bits = QA[:].rearrange("p h n -> p (h n)").bitcast(I32).rearrange(
            "p (o c w b) -> p o c w b", o=DT, c=PLANES, w=WORDS)
        w_low = xT
        w_lowT = wqT

        PT = stack.enter_context(nc.psum_tensor("PT", [P, 2, R * S], F32))
        PA = stack.enter_context(nc.psum_tensor("PA", [P, 2, 512], F32))
        PO = stack.enter_context(nc.psum_tensor("PO", [P, 512], F32))
        PM = stack.enter_context(nc.psum_tensor("PM", [P, 512], F32))

        def q_psum(o):
            return PT[:, o // 2, (o % 2) * N:(o % 2 + 1) * N]

        dq1 = nc.dram_tensor("dq1", (3, D, N), BF16, kind="Internal").ap()
        dk1 = nc.dram_tensor("dk1", (3, KV, N), BF16, kind="Internal").ap()
        dk2 = nc.dram_tensor("dk2", (3, KV, B * T2), BF16, kind="Internal").ap()
        dq2 = nc.dram_tensor("dq2", (NT, 3, D, P), BF16, kind="Internal").ap()

        ld_planes = sem("ld_planes")
        ld_x = sem("ld_x")
        ld_wq = sem("ld_wq")
        ld_wkv = sem("ld_wkv")
        ld_nat = sem("ld_nat")
        ld_wo = sem("ld_wo")
        ld_xn = sem("ld_xn")
        ld_ctx = sem("ld_ctx")
        ld_mask = sem("ld_mask")
        ld_lut = sem("ld_lut")
        const_ready = sem("const_ready")
        pool_own = sem("pool_own")
        dve_own = sem("dve_own")
        act_own = sem("act_own")
        bits_done = sem("bits_done")
        signs = sem("signs")
        scales = sem("scales")
        q_ready = sem("q_ready")
        sv_ready = sem("sv_ready")
        sv_done = sem("sv_done")
        q_out = sem("q_out")
        v_out = sem("v_out")
        q_split = sem("q_split")
        c_split = sem("c_split")
        v2_ready = sem("v2_ready")
        dq_written = sem("dq_written")
        dk_written = sem("dk_written")
        dc_written = sem("dc_written")
        qa_ready = sem("qa_ready")
        ka1_ready = sem("ka1_ready")
        ka2_ready = sem("ka2_ready")
        a_full = sem("a_full")
        sm_ready = sem("sm_ready")
        sub_done = sem("sub_done")
        t_full = sem("t_full")
        exp_done = sem("exp_done")
        pv_done = sem("pv_done")
        po_free = sem("po_free")
        pm_full = sem("pm_full")
        pm_free = sem("pm_free")
        o_ready = sem("o_ready")
        x1_ready = sem("x1_ready")
        x2_ready = sem("x2_ready")
        x1_cast = sem("x1_cast")
        x1_rest = sem("x1_rest")
        x1_split = sem("x1_split")
        parts_sent = sem("parts_sent")
        qa2_ready = sem("qa2_ready")
        w_ready = sem("w_ready")
        wT_ready = sem("wT_ready")
        var_ready = sem("var_ready")
        rstd_ready = sem("rstd_ready")
        y_ready = sem("y_ready")
        y_sent = sem("y_sent")

        block = stack.enter_context(nc.Block())

        def dma_tile(eng, dst, src, s):
            eng.dma_start(dst, src).then_inc(s, 16)

        @block.sync
        def _(sp):
            dma_tile(sp, planes[:], qweight[:, :, 0:PLANES, :], ld_planes)
            dma_tile(sp, xT[:], x_T.rearrange("(t p) n -> p t n", p=P), ld_x)
            dma_tile(sp, wqT[:], wq_T.rearrange("(t p) n -> p t n", p=P), ld_wq)
            dma_tile(sp, wkvT[:], wkv_T.rearrange("(t p) n -> p t n", p=P), ld_wkv)
            dma_tile(sp, x[:], x_tok.rearrange("(t p) d -> p t d", p=P), ld_xn)
            dma_tile(sp, woT[:], wo_T.rearrange("(t p) n -> p t n", p=P), ld_wo)
            dma_tile(sp, maskq[:], mask.rearrange("(t p) k -> p t k", p=P), ld_mask)
            dma_tile(sp, lut[:], lut4, ld_lut)
            sp.wait_ge(q_split, 1)
            for s in range(3):
                dma_tile(sp, dk1[s], k_parts[:, s, :], dk_written)
            sp.wait_ge(dk_written, 48)
            for s in range(SLOTS):
                dma_tile(sp, KA1[s * HD:(s + 1) * HD, :, :], dk1[K_PART[s]].rearrange("(g d) n -> d g n", d=HD), ka1_ready)
            for b in range(B):
                tok = slice(b * S, (b + 1) * S)
                sp.wait_ge(q_split, 2 + b)
                for s in range(3):
                    dma_tile(sp, dq1[s, :, tok].rearrange("(o p) n -> p o n", p=P), q_parts[:, s, :, tok], dq_written)
                sp.wait_ge(dq_written, 48 * (b + 1))
                if b == 0:
                    sp.wait_ge(bits_done, 1)
                for s in range(SLOTS):
                    dma_tile(sp, QA[s * HD:(s + 1) * HD, :, tok], dq1[Q_PART[s], :, tok].rearrange("(h d) n -> d h n", d=HD), qa_ready)
            sp.wait_ge(c_split, 1)
            for s in range(3):
                dma_tile(sp, dk2[s], c_parts[:, s, :], dc_written)
            sp.wait_ge(dc_written, 48)
            for s in range(SLOTS):
                dma_tile(sp, KA2[s * HD:(s + 1) * HD, :, :], dk2[K_PART[s]].rearrange("(g d) n -> d g n", d=HD), ka2_ready)
            for t in range(NT):
                sp.wait_ge(x1_split, t + 1)
                for s in range(3):
                    dma_tile(sp, dq2[t, s].rearrange("(o p) n -> p o n", p=P), parts[:, s], parts_sent)
                sp.wait_ge(parts_sent, 48 * (t + 1))
                sp.wait_ge(a_full, first_fill(G * (t // QT + 1)))
                for s in range(SLOTS):
                    dma_tile(sp, QA[s * HD:(s + 1) * HD, :, t * P:(t + 1) * P],
                             dq2[t, Q_PART[s]].rearrange("(h d) n -> d h n", d=HD), qa2_ready)
            for t in range(NT):
                sp.wait_ge(y_ready, t + 1)
                dma_tile(sp, out[t * P:(t + 1) * P, :], O[:, t, :], y_sent)
            sp.wait_ge(y_sent, 16 * NT)

        @block.gpsimd
        def _(pool):
            own = [0]

            def link(ins):
                own[0] += 1
                ins.then_inc(pool_own, 1)
                pool.wait_ge(pool_own, own[0])

            nc.gpsimd.memset(ones[:], 1.0)
            nc.gpsimd.memset(half[:], -0.5)
            link(nc.gpsimd.memset(ident[:], 0.0))
            nc.gpsimd.affine_select(out=ident[:], in_=ident[:], compare_op=ALU.not_equal, fill=1.0, base=0,
                                    pattern=[[-1, P]], channel_multiplier=1).then_inc(const_ready, 1)
            link(nc.gpsimd.memset(V1[:], 0.0))
            nc.gpsimd.memset(V1[:, :, :, HD:HD + 1], 1.0).then_inc(const_ready, 1)
            pool.wait_ge(ld_ctx, 32)
            link(nc.gpsimd.tensor_copy(c_parts[:, 0], cT))
            link(nc.gpsimd.tensor_tensor(cT, cT, c_parts[:, 0], ALU.subtract))
            link(nc.gpsimd.tensor_copy(c_parts[:, 1], cT))
            nc.gpsimd.tensor_tensor(c_parts[:, 2], cT, c_parts[:, 1], ALU.subtract).then_inc(c_split, 1)
            pool.wait_ge(dk_written, 48)
            link(nc.gpsimd.memset(V2[:], 0.0))
            link(nc.gpsimd.memset(V2[:, :, :, HD:HD + 1], 1.0))
            nc.gpsimd.tensor_copy(V2[:, :, :, 0:HD], cN.rearrange("p (t g d) -> p t g d", g=G, d=HD)).then_inc(v2_ready, 1)

            def shift(u):
                keys = key_tiles(u) * P
                for i in range(R * QT):
                    pool.wait_ge(sm_ready, R * QT * u + i + 1)
                    row = SM[:, u % SM_RING, i, 0:keys]
                    nc.gpsimd.tensor_scalar(row, row, -1.0, mx[:, u % SM_RING, i:i + 1], ALU.mult, ALU.add).then_inc(sub_done, 1)

            def side(what, t):
                if what in ("project_o", "norm_x2", "ffn"):
                    n = norm_count[0] = norm_count[0] + 1
                    pool.wait_ge(var_ready, n)
                    nc.gpsimd.tensor_tensor(rstd[:], var[:], half[:], ALU.pow).then_inc(rstd_ready, 1)

            norm_count = [0]
            shift(0)
            shift(1)
            for u in range(UNITS + 1):
                if u + 2 < UNITS:
                    shift(u + 2)
                for what, t in SIDE[u]:
                    side(what, t)

        @block.scalar
        def _(act):
            own = [0]

            def link(ins):
                own[0] += 1
                ins.then_inc(act_own, 1)
                act.wait_ge(act_own, own[0])

            dma_tile(act, wq_n, wq.rearrange("(t p) i -> p t i", p=P), ld_nat)
            dma_tile(act, wkv_n, wkv.rearrange("(t p) i -> p t i", p=P), ld_nat)
            dma_tile(act, scl[:, 0:10], scales_in, ld_nat)
            dma_tile(act, wo_n, wo.rearrange("(t p) i -> p t i", p=P), ld_nat)
            dma_tile(act, cT, ctx_T, ld_ctx)
            dma_tile(act, cN.rearrange("p (t d) -> p t d", d=KV), ctx.rearrange("(t p) d -> p t d", p=P), ld_ctx)
            dma_tile(act, biasb[:], bias.rearrange("(a o) -> a o", a=1).broadcast_to([P, D]), ld_lut)
            act.wait_ge(ld_wq, 16)
            nc.scalar.activation(wqT[:], wqT[:], ACT.Sign).then_inc(signs, 1)
            act.wait_ge(ld_wkv, 16)
            nc.scalar.activation(wkvT[:], wkvT[:], ACT.Sign).then_inc(signs, 1)
            act.wait_ge(scales, 1)
            act.wait_ge(q_ready, 1)
            nc.scalar.activation(kf, PA[:, 0, :], ACT.Copy, scale=scl[:, 4:5]).then_inc(q_out, 1)
            for o in range(DT):
                act.wait_ge(q_ready, 2 + o)
                nc.scalar.activation(qf[:, o], q_psum(o), ACT.Copy, scale=scl[:, o:o + 1]).then_inc(q_out, 1)
            act.wait_ge(ld_wo, 16)
            nc.scalar.activation(woT[:], woT[:], ACT.Sign).then_inc(signs, 1)

            def exps(u, k):
                c = first_chunk(u) + k
                act.wait_ge(t_full, c + 1)
                if c >= PT_RING:
                    act.wait_ge(pv_done, c - PT_RING + 1)
                else:
                    act.wait_ge(dq_written, 48 * B)
                nc.scalar.activation(PTs[:, c % PT_RING, :], PT[:, c % 2, :], ACT.Exp, scale=-1.0).then_inc(exp_done, 1)

            def unload(u):
                act.wait_ge(pv_done, first_chunk(u + 1))
                if u >= 1:
                    act.wait_ge(pm_full, PM_USE[("turn_unit", u - 1)] + 1)
                nc.scalar.activation(OT[:], PO[:, 0:S], ACT.Copy).then_inc(po_free, 1)

            def side(what, t):
                if what == "turn_o":
                    act.wait_ge(pm_full, PM_USE[(what, t)] + 1)
                    nc.scalar.activation(oT2[t % 2], PM[:].rearrange("p (o n) -> p o n", o=DT), ACT.Copy).then_inc(pm_free, 1)
                if what == "turn_x1":
                    act.wait_ge(pm_full, PM_USE[(what, t)] + 1)
                    if t > 0:
                        act.wait_ge(x1_split, t)
                        act.wait_ge(parts_sent, 48 * t)
                    nc.scalar.activation(xq[:], PM[:].rearrange("p (o n) -> p o n", o=DT), ACT.Copy, scale=0.25).then_inc(pm_free, 1)
                    act.wait_ge(pm_free, PM_USE[(what, t)] + 1)
                    nc.scalar.activation(parts[:, 0], xq[:], ACT.Copy).then_inc(x1_cast, 1)
                    act.wait_ge(x1_rest, t + 1)
                    nc.scalar.activation(parts[:, 1], xq[:], ACT.Copy).then_inc(x1_cast, 1)
                if what == "turn_x2":
                    act.wait_ge(pm_full, PM_USE[(what, t)] + 1)
                    nc.scalar.activation(oT2[t % 2], PM[:].rearrange("p (o n) -> p o n", o=DT), ACT.Copy).then_inc(pm_free, 1)
                if what == "turn_w":
                    act.wait_ge(pm_full, PM_USE[(what, t)] + 1)
                    nc.scalar.activation(w_lowT[:, :, t * P:(t + 1) * P], PM[:].rearrange("p (i n) -> p i n", i=DT), ACT.Copy).then_inc(pm_free, 1)

            oT2 = (oT[:], x2T[:])
            for u in range(UNITS + 1):
                if u < UNITS:
                    exps(u, 0)
                if u >= 1:
                    unload(u - 1)
                if u < UNITS:
                    for k in range(1, key_tiles(u)):
                        exps(u, k)
                for what, t in SIDE[u]:
                    side(what, t)

        @block.vector
        def _(dve):
            own = [0]

            def link(ins):
                own[0] += 1
                ins.then_inc(dve_own, 1)
                dve.wait_ge(dve_own, own[0])

            vec = nc.vector
            dve.wait_ge(ld_planes, 16)
            for i in range(BITS):
                ins = vec.tensor_scalar(bits[:, :, :, :, i].rearrange("p o c w -> p (o c w)"),
                                        planes[:].rearrange("p o c w -> p (o c w)"), i, 1,
                                        ALU.logical_shift_right, ALU.bitwise_and)
            link(ins)
            plane = [bits[:, :, c].rearrange("p o w b -> p o (w b)") for c in range(PLANES)]
            vec.scalar_tensor_tensor(out=code[:, 0], in0=plane[1], scalar=2.0, in1=plane[0], op0=ALU.mult, op1=ALU.add)
            link(vec.scalar_tensor_tensor(out=code[:, 1], in0=plane[3], scalar=2.0, in1=plane[2], op0=ALU.mult, op1=ALU.add))
            vec.scalar_tensor_tensor(out=idx[:], in0=code[:, 1], scalar=4.0, in1=code[:, 0], op0=ALU.mult,
                                     op1=ALU.add).then_inc(bits_done, 1)
            dve.wait_ge(ld_nat, 16 * 4)
            vec.tensor_reduce(mean[:, 0:4], wq_n, AX.X, ALU.add, apply_absolute_value=True)
            link(vec.tensor_reduce(mean[:, 4:6], wkv_n, AX.X, ALU.add, apply_absolute_value=True))
            link(vec.tensor_scalar(mean[:, 0:6], mean[:, 0:6], 1.0 / D, 1e-8, ALU.mult, ALU.max))
            link(vec.tensor_tensor(scl[:, 0:6], scl[:, 0:6], mean[:, 0:6], ALU.mult))
            vec.tensor_scalar(scl[:, 0:4], scl[:, 0:4], HD ** -0.5, None, ALU.mult).then_inc(scales, 1)
            dve.wait_ge(const_ready, 1)
            vec.tensor_scalar(diag[:, DT, :], ident[:], scl[:, 5:6], None, ALU.mult).then_inc(scales, 1)

            def split(src, dst, done):
                link(vec.tensor_copy(dst[0], src))
                link(vec.tensor_tensor(src, src, dst[0], ALU.subtract))
                link(vec.tensor_copy(dst[1], src))
                vec.tensor_tensor(dst[2], src, dst[1], ALU.subtract).then_inc(done, 1)

            dve.wait_ge(q_out, 1)
            split(kf, [k_parts[:, s] for s in range(3)], q_split)
            dve.wait_ge(q_out, 1 + DT)
            for b in range(B):
                tok = slice(b * S, (b + 1) * S)
                split(qf[:, :, tok], [q_parts[:, s, :, tok] for s in range(3)], q_split)
            dve.wait_ge(sv_ready, 1)
            vec.tensor_copy(sv[:], PM[:, 0:KV]).then_inc(sv_done, 1)
            dve.wait_ge(sv_done, 1)
            dve.wait_ge(const_ready, 2)
            dve.wait_ge(q_ready, 2 + DT)
            for t in range(NT):
                vec.tensor_tensor(V1[:, t, :, 0:HD], PA[:, 1, t * KV:(t + 1) * KV].rearrange("p (g d) -> p g d", g=G),
                                  sv[:].rearrange("p (g d) -> p g d", g=G), ALU.mult).then_inc(v_out, 1)
            link(vec.tensor_reduce(mean[:, 6:10], wo_n, AX.X, ALU.add, apply_absolute_value=True))
            link(vec.tensor_scalar(mean[:, 6:10], mean[:, 6:10], 1.0 / D, 1e-8, ALU.mult, ALU.max))
            link(vec.tensor_tensor(scl[:, 6:10], scl[:, 6:10], mean[:, 6:10], ALU.mult))
            for o in range(DT):
                ins = vec.tensor_scalar(diag[:, o, :], ident[:], scl[:, 6 + o:7 + o], None, ALU.mult)
            ins.then_inc(scales, 1)
            dve.wait_ge(sv_ready, 2)
            vec.tensor_copy(so[:], PO[:]).then_inc(sv_done, 1)
            dve.wait_ge(c_split, 1)
            dve.wait_ge(v2_ready, 1)

            def weights():
                dve.wait_ge(ld_lut, 32)
                dve.wait_ge(q_ready, 2 + DT)
                for j in range(LUT):
                    yield link(vec.tensor_scalar(code[:, j % 2], idx[:], float(j), None, ALU.is_equal))
                    for o in range(DT):
                        entry = lut[:, o, j:j + 1]
                        if j == 0:
                            ins = vec.tensor_scalar(w_low[:, o], code[:, 0, o], entry, None, ALU.mult)
                        else:
                            ins = vec.scalar_tensor_tensor(out=w_low[:, o], in0=code[:, j % 2, o], scalar=entry,
                                                           in1=w_low[:, o], op0=ALU.mult, op1=ALU.add)
                        if j == LUT - 1:
                            ins.then_inc(w_ready, 1)
                            yield
                        else:
                            yield link(ins) if o == DT - 1 else ins

            def maxima(u, i):
                f = first_fill(u) + i
                dve.wait_ge(a_full, f + 1)
                if u >= SM_RING:
                    dve.wait_ge(t_full, first_chunk(u - SM_RING + 1))
                if layer(u):
                    vec.tensor_tensor_reduce(SM[:, u % SM_RING, i, :], PA[:, f % 2, :], maskq[:, i % QT, :], 1.0, LOWEST,
                                             ALU.add, ALU.max, mx[:, u % SM_RING, i:i + 1]).then_inc(sm_ready, 1)
                else:
                    for q in range(QT):
                        vec.tensor_scalar(SM[:, u % SM_RING, QT * i + q, 0:S], PA[:, f % 2, q * S:(q + 1) * S], 1.0, None,
                                          ALU.mult, ALU.max, accum_out=mx[:, u % SM_RING, QT * i + q:QT * i + q + 1]).then_inc(sm_ready, 1)

            def normalise(u):
                n = PM_USE[("turn_unit", u)]
                if u == 0:
                    dve.wait_ge(dc_written, 48)
                dve.wait_ge(pm_full, n + 1)
                pm = PM[:, 0:QT * P].rearrange("p (q r v) -> p q r v", q=QT, r=R)
                link(vec.reciprocal(rsum[:], pm[:, :, :, HD:HD + 1]))
                t = batch(u) * QT
                for q in range(QT):
                    ins = vec.tensor_tensor(
                        O[:, t + q, group(u) * R * HD:(group(u) + 1) * R * HD].rearrange("p (r d) -> p r d", r=R),
                        pm[:, q, :, 0:HD], rsum[:, q].broadcast_to([P, R, HD]), ALU.mult)
                ins.then_inc(pm_free, 1)
            norm_count = [0]

            def layernorm(src, dst, ready, t):
                n = norm_count[0] = norm_count[0] + 1
                link(vec.bn_stats(stats[:], src))
                link(vec.bn_aggr(mv[:], stats[:]))
                vec.tensor_scalar(var[:], mv[:, 1:2], EPS, None, ALU.add).then_inc(var_ready, 1)
                dve.wait_ge(rstd_ready, n)
                vec.tensor_scalar(dst, src, mv[:, 0:1], rstd[:], ALU.subtract, ALU.mult).then_inc(ready, 1)
                dve.wait_ge(ready, t + 1)

            def side(what, t):
                if what == "project_o":
                    dve.wait_ge(pm_full, PM_USE[(what, t)] + 1)
                    vec.tensor_tensor(tmp[:], PM[:], so[:], ALU.mult).then_inc(pm_free, 1)
                    dve.wait_ge(pm_free, PM_USE[(what, t)] + 1)
                    link(vec.tensor_tensor(tmp[:], tmp[:], x[:, t], ALU.add))
                    layernorm(tmp[:], x[:, t], x1_ready, t)
                if what == "turn_x1":
                    dve.wait_ge(x1_cast, 2 * t + 1)
                    vec.tensor_tensor(xq[:], xq[:], parts[:, 0], ALU.subtract).then_inc(x1_rest, 1)
                    dve.wait_ge(x1_cast, 2 * t + 2)
                    vec.tensor_tensor(parts[:, 2], xq[:], parts[:, 1], ALU.subtract).then_inc(x1_split, 1)
                if what == "norm_x2":
                    last_unit = B * G + (t // QT + 1) * G - 1
                    dve.wait_ge(pm_free, PM_USE[("turn_unit", last_unit)] + 1)
                    link(vec.tensor_tensor(tmp[:], O[:, t], x[:, t], ALU.add))
                    layernorm(tmp[:], x[:, t], x2_ready, t)
                if what == "ffn":
                    dve.wait_ge(x2_ready, t + 1)
                    link(vec.tensor_tensor(tmp[:], x[:, t], biasb[:], ALU.add))
                    dve.wait_ge(pm_full, PM_USE[(what, t)] + 1)
                    vec.tensor_tensor(tmp[:], tmp[:], PM[:], ALU.add).then_inc(pm_free, 1)
                    dve.wait_ge(pm_free, PM_USE[(what, t)] + 1)
                    layernorm(tmp[:], O[:, t], y_ready, t)

            work = weights()
            dve.wait_ge(ld_xn, 16)
            dve.wait_ge(ld_mask, 16)
            for u in (0, 1):
                for i in range(fills(u)):
                    maxima(u, i)
            for u in range(UNITS + 1):
                if u + 2 < UNITS:
                    for i in range(fills(u + 2)):
                        maxima(u + 2, i)
                        if layer(u) and i % 2:
                            next(work, None)
                next(work, None)
                if u >= 1:
                    normalise(u - 1)
                if u == 3 * G:
                    for _ in work:
                        pass
                for what, t in SIDE[u]:
                    side(what, t)

        @block.tensor
        def _(pe):
            mm = nc.tensor.matmul
            pe.wait_ge(ld_x, 16)
            pe.wait_ge(signs, 2)
            for i in range(DT):
                last = mm(PA[:, 0, :], wkvT[:, i, 0:KV], xT[:, i, :], start=(i == 0), stop=(i == DT - 1))
            last.then_inc(q_ready, 1)
            for o in range(DT):
                for i in range(DT):
                    last = mm(q_psum(o), wqT[:, i, o * P:(o + 1) * P], xT[:, i, :], start=(i == 0), stop=(i == DT - 1))
                last.then_inc(q_ready, 1)
            for t in range(NT):
                for i in range(DT):
                    last = mm(PA[:, 1, t * KV:(t + 1) * KV], xT[:, i, t * P:(t + 1) * P], wkvT[:, i, KV:2 * KV],
                              start=(i == 0), stop=(i == DT - 1))
            last.then_inc(q_ready, 1)
            pe.wait_ge(scales, 2)
            pe.wait_ge(const_ready, 1)
            mm(PM[:, 0:KV], ones[:], diag[:, DT, :], start=True, stop=True).then_inc(sv_ready, 1)
            pe.wait_ge(scales, 3)
            for o in range(DT):
                last = mm(PO[:, o * P:(o + 1) * P], ones[:], diag[:, o, :], start=True, stop=True)
            last.then_inc(sv_ready, 1)

            def scores(u, i):
                f = first_fill(u) + i
                b, g = batch(u), group(u)
                if i == 0:
                    if layer(u):
                        pe.wait_ge(ka2_ready, 16 * SLOTS)
                        pe.wait_ge(qa2_ready, 16 * SLOTS * QT * (b + 1))
                    else:
                        pe.wait_ge(ka1_ready, 16 * SLOTS)
                        pe.wait_ge(qa_ready, 16 * SLOTS * (b + 1))
                if f >= 2:
                    pe.wait_ge(sm_ready, scored(f - 2))
                elif f == 0:
                    pe.wait_ge(q_out, 1)
                else:
                    pe.wait_ge(v_out, NT)
                if layer(u):
                    h, q = g * R + i // QT, i % QT
                    tok = b * S + q * P
                    last = mm(PA[:, f % 2, :], QA[0:KR, h, tok:tok + P], KA2[0:KR, g, b * T2:(b + 1) * T2], start=True, stop=True)
                else:
                    for q in range(QT):
                        tok = b * S + q * P
                        last = mm(PA[:, f % 2, q * S:(q + 1) * S], QA[0:KR, g * R + i, tok:tok + P],
                                  KA1[0:KR, g, b * S:(b + 1) * S], start=True, stop=True)
                last.then_inc(a_full, 1)

            def scored(f):
                n = first_fill(B * G)
                return QT * (f + 1) if f < n else QT * n + f + 1 - n

            def turn(u, k):
                c = first_chunk(u) + k
                if c < 2:
                    pe.wait_ge(q_out, 1 + DT)
                else:
                    pe.wait_ge(exp_done, c - 1)
                for i in range(R * QT):
                    if k == 0:
                        pe.wait_ge(sub_done, R * QT * u + i + 1)
                    last = nc.tensor.transpose(PT[:, c % 2, i * P:(i + 1) * P],
                                               SM[:, u % SM_RING, i, k * P:(k + 1) * P], ident[:])
                last.then_inc(t_full, 1)

            def product(u, k):
                c = first_chunk(u) + k
                pe.wait_ge(exp_done, c + 1)
                if k == 0 and u == 0:
                    pe.wait_ge(sv_done, 2)
                if k == 0 and u >= 1:
                    pe.wait_ge(po_free, u)
                V = V2 if layer(u) else V1
                if u == B * G and k == 0:
                    pe.wait_ge(v2_ready, 1)
                for r in range(R):
                    last = mm(PO[VW * r:VW * (r + 1), 0:S], V[:, batch(u) * key_tiles(u) + k, group(u), :],
                              PTs[:, c % PT_RING, r * S:(r + 1) * S], start=(k == 0), stop=(k == key_tiles(u) - 1),
                              tile_position=(0, VW * r))
                last.then_inc(pv_done, 1)

            def pm_claim(n):
                if n == 0:
                    pe.wait_ge(sv_done, 1)
                else:
                    pe.wait_ge(pm_free, n)

            def turn_unit(u):
                pe.wait_ge(po_free, u + 1)
                pm_claim(PM_USE[("turn_unit", u)])
                for q in range(QT):
                    last = nc.tensor.transpose(PM[:, q * P:(q + 1) * P], OT[:, q * P:(q + 1) * P], ident[:])
                last.then_inc(pm_full, 1)

            def side(what, t):
                if what == "norm_x2":
                    return
                n = PM_USE[(what, t)]
                tile = oT if t % 2 == 0 else x2T
                if what == "turn_o":
                    u = (t // QT + 1) * G - 1
                    pe.wait_ge(pm_free, PM_USE[("turn_unit", u)] + 1)
                    pm_claim(n)
                    for i in range(DT):
                        last = nc.tensor.transpose(PM[:, i * P:(i + 1) * P], O[:, t, i * P:(i + 1) * P], ident[:])
                if what == "project_o":
                    pe.wait_ge(signs, 3)
                    pe.wait_ge(pm_free, PM_USE[("turn_o", t)] + 1)
                    pm_claim(n)
                    for i in range(DT):
                        last = mm(PM[:], tile[:, i, :], woT[:, i, :], start=(i == 0), stop=(i == DT - 1))
                if what == "turn_x1":
                    pe.wait_ge(x1_ready, t + 1)
                    pm_claim(n)
                    for i in range(DT):
                        last = nc.tensor.transpose(PM[:, i * P:(i + 1) * P], x[:, t, i * P:(i + 1) * P], ident[:])
                if what == "turn_x2":
                    pe.wait_ge(x2_ready, t + 1)
                    pm_claim(n)
                    for i in range(DT):
                        last = nc.tensor.transpose(PM[:, i * P:(i + 1) * P], x[:, t, i * P:(i + 1) * P], ident[:])
                if what == "turn_w":
                    pe.wait_ge(w_ready, t + 1)
                    pm_claim(n)
                    for i in range(DT):
                        last = nc.tensor.transpose(PM[:, i * P:(i + 1) * P], w_low[:, t, i * P:(i + 1) * P], ident[:])
                if what == "ffn":
                    pe.wait_ge(pm_free, max(PM_USE[("turn_x2", t)], PM_USE[("turn_w", DT - 1)]) + 1)
                    pm_claim(n)
                    for i in range(DT):
                        last = mm(PM[:], tile[:, i, :], w_lowT[:, i, :], start=(i == 0), stop=(i == DT - 1))
                last.then_inc(pm_full, 1)

            for u in (0, 1):
                for i in range(fills(u)):
                    scores(u, i)
            for u in range(UNITS):
                per = fills(u + 2) // key_tiles(u) if u + 2 < UNITS else 0
                for k in range(key_tiles(u)):
                    turn(u, k)
                    for i in range(k * per, fills(u + 2) if k == key_tiles(u) - 1 and per else (k + 1) * per):
                        scores(u + 2, i)
                    if k >= 1:
                        product(u, k - 1)
                    elif u >= 1:
                        product(u - 1, key_tiles(u - 1) - 1)
                if u >= 1:
                    turn_unit(u - 1)
                for what, t in SIDE[u]:
                    side(what, t)
            product(UNITS - 1, key_tiles(UNITS - 1) - 1)
            turn_unit(UNITS - 1)
            for what, t in SIDE[UNITS]:
                side(what, t)


_OUT = ((B, S, D), "float32")


def kernel(**inputs):
    import numpy as np
    import concourse.bacc as bacc
    from concourse.bass_utils import run_bass_kernel_spmd

    a = {k: np.asarray(v) for k, v in inputs.items()}
    x = a["x"].reshape(N, D)
    wk, wv = a["L0_attn_k_weight"], a["L0_attn_v_weight"]
    wkv = np.concatenate([wk, wv], axis=0)
    ctx = a["ctx_1024"].reshape(B * T2, KV)
    lay = {
        "x_tok": x, "x_T": x.T, "wq_T": a["L0_attn_q_weight"].T, "wq": a["L0_attn_q_weight"],
        "wkv_T": wkv.T, "wkv": wkv, "wo_T": a["L0_attn_o_weight"].T, "wo": a["L0_attn_o_weight"],
        "scales": np.concatenate([a[f"L0_attn_{n}_scale"].reshape(-1, P).T for n in "qkvo"], axis=1),
        "ctx": ctx, "ctx_T": ctx.T, "mask": a["mask_SxS2_ff0"],
        "qweight": a["L0_ffn_qweight"].reshape(8, DT, P, WORDS).transpose(2, 1, 0, 3),
        "lut4": a["L0_ffn_lut4"].reshape(DT, P, LUT).transpose(1, 0, 2), "lut8": a["L0_ffn_lut8"], "bias": a["L0_ffn_bias"],
    }
    nc = bacc.Bacc("TRN2", target_bir_lowering=False, num_devices=1)
    arrays, args = {}, []
    for name, v in lay.items():
        v = np.ascontiguousarray(v)
        arrays[f"in_{name}"] = v
        args.append(nc.dram_tensor(f"in_{name}", v.shape, mybir.dt.from_np(v.dtype), kind="ExternalInput").ap())
    out = nc.dram_tensor("out_0", (N, D), F32, kind="ExternalOutput").ap()
    kernel_body(nc, *args, out)
    r = run_bass_kernel_spmd(nc, [arrays], core_ids=[0])
    return r.results[0]["out_0"].reshape(B, S, D)
```

```python
from contextlib import ExitStack

import concourse.bass as bass
from concourse import mybir

F32 = mybir.dt.float32
BF16 = mybir.dt.bfloat16
I32 = mybir.dt.int32
U8 = mybir.dt.uint8
ALU = mybir.AluOpType
ACT = mybir.ActivationFunctionType
AX = mybir.AxisListType

P = 128
B, S, D = 2, 256, 512
T2 = 512
H, G, HD = 32, 8, 16
R = H // G
N = B * S
NT = N // P
DT = D // P
QT = S // P
KV = G * HD
VW = 32
Q_PART = (0, 0, 1, 1, 0, 2)
K_PART = (0, 1, 0, 1, 2, 0)
SLOTS = len(Q_PART)
KR = SLOTS * HD
EPS = 1e-5
LOWEST = -3.4e38
LUT = 16
PLANES = 4
Q_STEPS = 5
AHEAD = 5
LEAVES = 6
BITS = 32
WORDS = D // BITS
NORM2 = 64.0 * 64.0

STEPS = (4, 2)

UNITS = 2 * B * G
SM_RING = 3
PT_RING = 3
T_RING = 3
Q_SENDS = ((0, 0, 1), (0, 1, 2), (0, 2, 4), (1, 0, 4))
Q_WRITES = (16, 32, 64, 80)
Q_FIRST = 3


def layer(u):
    return u // (B * G)


def batch(u):
    return u // G % B


def group(u):
    return u % G


def key_tiles(u):
    return (T2 if layer(u) else S) // P


def first_chunk(u):
    return sum(key_tiles(v) for v in range(u))


def fills(u):
    return R * QT if layer(u) else R


def row_block(u, i):
    return i % R * QT + i // R


def first_fill(u):
    return sum(fills(v) for v in range(u))


def table_plan():
    steps, fills_, free_at, merges = [], [], [(i, 0) for i in range(LEAVES)], 0
    for o in range(DT):
        held = []
        for n in range(LUT // 2):
            place, after = (-1, 0) if n == 0 else free_at.pop(0)
            fills_.append((o, n, place, after))
            steps.append(("leaf", o, n, place))
            held.append((0, place))
            while len(held) > 1 and held[-1][0] == held[-2][0]:
                level, source = held.pop()
                into = held.pop()[1]
                merges += 1
                steps.append(("merge", o, level + 1, into, source))
                free_at.append((source, merges))
                held.append((level + 1, into))
    return steps, fills_


def table_pace():
    steps, _ = table_plan()
    pace, left = {}, Q_STEPS + len(steps)
    for u in range(UNITS):
        for k in range(key_tiles(u)):
            busy = u in (G + 1, G + 2) and k == 0 or layer(u) and k == 3
            pace[first_chunk(u) + k] = n = min(left, 0 if busy else 1)
            left -= n
    assert left == 0
    fill_pace, done, n = {}, -Q_STEPS, 0
    kinds = [s[0] for s in steps]
    for c in sorted(pace):
        done += pace[c]
        due = sum(k == "leaf" for k in kinds[:max(done + AHEAD, 0)])
        fill_pace[c] = due - n
        n = due
    return pace, fill_pace


def kernel_body(nc, x_tok, x_T, wq_T, wkv_T, wo_T, scales_in, v_scale, o_scale,
                ctx, ctx_T, mask, qweight, lut4, lut8, bias, out):
    SIDE = {c: [] for c in range(first_chunk(UNITS) + 1)}
    def side_at(c, what, t):
        SIDE[c].append((what, t))

    for b in range(B):
        for n, t in enumerate(range(b * QT, (b + 1) * QT)):
            at = first_chunk(G * (b + 1) + 1)
            side_at(at + 2 * n, "turn_o", t)
            side_at(at + 2 * n + 1, "project_o", t)
            side_at(at + 4 + 2 * n + b, "turn_x1", t)
            at = first_chunk(B * G + G * (b + 1) + 1) if b < B - 1 else first_chunk(UNITS)
            late = b < B - 1
            side_at(at, "norm_x2", t)
            side_at(at + (6 + 2 * n) * late, "turn_x2", t)
            side_at(at + (4 * 4 + 2 * n) * late, "ffn", t)
    SIDE[first_chunk(UNITS)].sort(key=lambda s: ("norm_x2", "turn_x2", "ffn").index(s[0]))
    for o in range(DT):
        side_at(first_chunk(3 * G + 4) + o, "turn_w", o)
    STEPS_LOW, FILLS_LOW = table_plan()
    PACE, FILL_PACE = table_pace()
    order = [s for c in sorted(SIDE) for s in SIDE[c] if s[0] != "norm_x2"]
    PS_USE = {what: n for n, what in enumerate(order)}

    with ExitStack() as stack:
        def sb(name, shape, dt=F32):
            return stack.enter_context(nc.sbuf_tensor(name, shape, dt))

        def sem(name):
            return stack.enter_context(nc.semaphore(name))

        ident = sb("ident", [P, P])
        ones = sb("ones", [P, P])
        xT = sb("xT", [P, DT, N])
        wqT = sb("wqT", [P, DT, D])
        wkvT = sb("wkvT", [P, DT, 2 * KV])
        woT = sb("woT", [P, DT, D])
        x = sb("x", [P, NT, D])
        O = sb("O", [P, NT, D])
        QA = sb("QA", [P, H, N], BF16)
        KA1 = sb("KA1", [P, G, N], BF16)
        KA2 = sb("KA2", [P, G, B * T2], BF16)
        V1 = sb("V1", [P, NT, G, VW])
        V2 = sb("V2", [P, B * T2 // P, G, VW])
        SM = sb("SM", [P, SM_RING, R * QT, T2])
        PTs = sb("PTs", [P, PT_RING, R * S])
        maskq = sb("maskq", [P, QT, T2])
        mx = sb("mx", [P, SM_RING, R * QT])
        rsum = sb("rsum", [P, QT, R, 1])
        masks = sb("masks", [P, DT, PLANES, WORDS, 8], I32)
        leaf = sb("leaf", [P, LEAVES - DT, D])
        lut = sb("lut", [P, DT, LUT])
        vo_scales = maskq[:].rearrange("p q t -> p (q t)")[:, 0:KV + D]
        planes = sb("planes", [P, DT, PLANES, WORDS], I32)
        scl = sb("scl", [P, DT + 1])
        wsum = sb("wsum", [P, DT + 1])
        biasb = sb("biasb", [P, D])
        oT = sb("oT", [P, DT, P])
        xq = sb("xq", [P, 2, DT, P])
        parts = sb("parts", [P, 3, DT, P], BF16)
        tmp = sb("tmp", [P, D])
        stats = sb("stats", [P, 6])
        mv = sb("mv", [P, 2])
        var = sb("var", [P, 1])
        root = sb("root", [P, 4])
        def free(slot, start, size):
            return SM[:, slot].rearrange("p a t -> p (a t)")[:, start:start + size]

        wq_raw = free(0, 0, DT * D).rearrange("p (i o) -> p i o", i=DT)
        wkv_raw = free(0, DT * D, DT * 2 * KV).rearrange("p (i o) -> p i o", i=DT)
        abs_q = free(0, DT * (D + 2 * KV), D)
        abs_kv = free(0, DT * (D + 2 * KV) + D, 2 * KV)
        wo_raw = free(1, 0, DT * D).rearrange("p (i o) -> p i o", i=DT)
        cT = free(1, DT * D, B * T2)
        cN = free(1, DT * D + B * T2, B * T2)
        qf = (free(2, 0, DT * S).rearrange("p (o n) -> p o n", o=DT), SM[:, 2, DT:2 * DT, S:T2])
        kf = free(2, 2 * T2, N)
        abs_o = SM[:, 0, 0:D // S, S:T2]
        sv = free(2, 3 * T2, KV)
        so = tmp[:]
        pt_flat = PTs[:].rearrange("p a t -> p (a t)").bitcast(BF16)
        q_parts = [flat[:, 0:3 * DT * S].rearrange("p (s o n) -> p s o n", s=3, o=DT)
                   for flat in (pt_flat, x[:].rearrange("p t d -> p (t d)").bitcast(BF16))]
        k_parts = V2[:].rearrange("p a g v -> p (a g v)").bitcast(BF16)[:, 0:3 * N].rearrange("p (s n) -> p s n", s=3)
        c_parts = O[:].rearrange("p a d -> p (a d)").bitcast(BF16)[:, 0:3 * B * T2].rearrange("p (s n) -> p s n", s=3)
        bit = masks[:].rearrange("p o c w b -> p o c (w b)").bitcast(U8).rearrange("p o c (w b k) -> p o c w k b", w=WORDS, k=4)
        OT = wkvT[:, 0, :]
        x2T = wkvT[:, 1:3, :].rearrange("p a (b n) -> p (a b) n", n=P)
        w_low = xT

        def place(n, o):
            return w_low[:, o] if n < 0 else wqT[:, n] if n < DT else leaf[:, n - DT]

        def inputs(row):
            return row.rearrange("p (w k b) -> p w k b", w=WORDS, k=4)

        w_lowT = wqT

        PT = stack.enter_context(nc.psum_tensor("PT", [P, T_RING, 512], F32))
        PA = stack.enter_context(nc.psum_tensor("PA", [P, 2, 512], F32))
        PO = stack.enter_context(nc.psum_tensor("PO", [P, 512], F32))
        PM = stack.enter_context(nc.psum_tensor("PM", [P, 512], F32))
        PS = stack.enter_context(nc.psum_tensor("PS", [P, 512], F32))

        def q_psum(b, o):
            bank = 2 * b + o // 2
            return (PS[:] if bank == 3 else PT[:, bank, :])[:, (o % 2) * S:(o % 2 + 1) * S]

        dq1 = nc.dram_tensor("dq1", (B, 3, D, S), BF16, kind="Internal").ap()
        dk1 = nc.dram_tensor("dk1", (3, KV, N), BF16, kind="Internal").ap()
        dk2 = nc.dram_tensor("dk2", (3, KV, B * T2), BF16, kind="Internal").ap()
        dq2 = nc.dram_tensor("dq2", (NT, 3, D, P), BF16, kind="Internal").ap()

        ld_planes = sem("ld_planes")
        ld_x = sem("ld_x")
        ld_wq = sem("ld_wq")
        ld_wkv = sem("ld_wkv")
        ld_scales = sem("ld_scales")
        ld_wo = sem("ld_wo")
        ld_xn = sem("ld_xn")
        ld_ctx = sem("ld_ctx")
        ld_mask = sem("ld_mask")
        ld_lut = sem("ld_lut")
        const_ready = sem("const_ready")
        pool_own = sem("pool_own")
        dve_own = sem("dve_own")
        act_own = sem("act_own")
        leaf_filled = sem("leaf_filled")
        merged = sem("merged")
        signs = sem("signs")
        abs_ready = sem("abs_ready")
        sums_ready = sem("sums_ready")
        scales = sem("scales")
        wo_scaled = sem("wo_scaled")
        q_ready = sem("q_ready")
        q_out = sem("q_out")
        v_out = sem("v_out")
        q_split = sem("q_split")
        c_split = sem("c_split")
        v2_ready = sem("v2_ready")
        dq_written = sem("dq_written")
        dk_written = sem("dk_written")
        dc_written = sem("dc_written")
        qa_ready = sem("qa_ready")
        ka1_ready = sem("ka1_ready")
        ka2_ready = sem("ka2_ready")
        a_full = sem("a_full")
        sm_ready = sem("sm_ready")
        sub_done = sem("sub_done")
        t_full = sem("t_full")
        exp_done = sem("exp_done")
        pv_done = sem("pv_done")
        po_free = sem("po_free")
        pm_full = sem("pm_full")
        pm_free = sem("pm_free")
        ps_full = sem("ps_full")
        ps_free = sem("ps_free")
        x1_ready = sem("x1_ready")
        x2_ready = sem("x2_ready")
        x1_split = sem("x1_split")
        parts_sent = sem("parts_sent")
        qa2_ready = sem("qa2_ready")
        y_ready = sem("y_ready")
        y_sent = sem("y_sent")

        block = stack.enter_context(nc.Block())

        def dma_tile(eng, dst, src, s):
            eng.dma_start(dst, src).then_inc(s, 16)

        @block.sync
        def _(sp):
            dma_tile(sp, wkv_raw, wkv_T.rearrange("(t p) n -> p t n", p=P), ld_wkv)
            dma_tile(sp, xT[:], x_T.rearrange("(t p) n -> p t n", p=P), ld_x)
            dma_tile(sp, wq_raw, wq_T.rearrange("(t p) n -> p t n", p=P), ld_wq)
            dma_tile(sp, cT, ctx_T, ld_ctx)
            dma_tile(sp, cN.rearrange("p (t d) -> p t d", d=KV), ctx.rearrange("(t p) d -> p t d", p=P), ld_ctx)
            dma_tile(sp, wo_raw, wo_T.rearrange("(t p) n -> p t n", p=P), ld_wo)
            dma_tile(sp, lut[:], lut4, ld_lut)
            dma_tile(sp, biasb[:], bias.rearrange("(a o) -> a o", a=1).broadcast_to([P, D]), ld_lut)
            sp.wait_ge(q_split, 1)
            dma_tile(sp, dk1.rearrange("s p n -> p s n"), k_parts, dk_written)
            sp.wait_ge(dk_written, 16)
            for s in range(SLOTS):
                dma_tile(sp, KA1[s * HD:(s + 1) * HD, :, :], dk1[K_PART[s]].rearrange("(g d) n -> d g n", d=HD), ka1_ready)

            def send_q(n):
                b, o0, o1 = Q_SENDS[n]
                sp.wait_ge(q_split, 2 + n)
                feats, heads, toks = slice(o0 * P, o1 * P), slice(o0 * P // HD, o1 * P // HD), slice(b * S, (b + 1) * S)
                if (o0, o1) == (0, DT):
                    dma_tile(sp, dq1[b].rearrange("s (o p) n -> p (s o) n", p=P), q_parts[b].rearrange("p s o n -> p (s o) n"), dq_written)
                else:
                    for o in range(o0, o1):
                        dma_tile(sp, dq1[b, :, o * P:(o + 1) * P].rearrange("s p n -> p s n"), q_parts[b][:, :, o], dq_written)
                sp.wait_ge(dq_written, Q_WRITES[n])
                for s in range(SLOTS):
                    dma_tile(sp, QA[s * HD:(s + 1) * HD, heads, toks],
                             dq1[b, Q_PART[s], feats].rearrange("(h d) n -> d h n", d=HD), qa_ready)

            for n in range(Q_FIRST):
                send_q(n)
            sp.wait_ge(c_split, 1)
            dma_tile(sp, dk2.rearrange("s p n -> p s n"), c_parts, dc_written)
            sp.wait_ge(scales, 4)
            dma_tile(sp, maskq[:], mask.rearrange("(t p) k -> p t k", p=P), ld_mask)
            for n in range(Q_FIRST, len(Q_SENDS)):
                send_q(n)
            dma_tile(sp, x[:], x_tok.rearrange("(t p) d -> p t d", p=P), ld_xn)
            sp.wait_ge(dc_written, 16)
            for s in range(SLOTS):
                dma_tile(sp, KA2[s * HD:(s + 1) * HD, :, :], dk2[K_PART[s]].rearrange("(g d) n -> d g n", d=HD), ka2_ready)
            for t in range(NT):
                sp.wait_ge(x1_split, t + 1)
                dma_tile(sp, dq2[t].rearrange("s (o p) n -> p (s o) n", p=P), parts[:].rearrange("p s o n -> p (s o) n"), parts_sent)
                sp.wait_ge(parts_sent, 16 * (t + 1))
                sp.wait_ge(a_full, first_fill(G * (t // QT + 1)))
                for s in range(SLOTS):
                    dma_tile(sp, QA[s * HD:(s + 1) * HD, :, t * P:(t + 1) * P],
                             dq2[t, Q_PART[s]].rearrange("(h d) n -> d h n", d=HD), qa2_ready)
            for t in range(NT):
                sp.wait_ge(y_ready, t + 1)
                dma_tile(sp, out[t * P:(t + 1) * P, :], O[:, t, :], y_sent)
            sp.wait_ge(y_sent, 16 * NT)

        @block.gpsimd
        def _(pool):
            own = [0]

            def link(ins):
                own[0] += 1
                ins.then_inc(pool_own, 1)
                pool.wait_ge(pool_own, own[0])

            nc.gpsimd.memset(ones[:], 1.0)
            link(nc.gpsimd.memset(ident[:], 0.0))
            nc.gpsimd.affine_select(out=ident[:], in_=ident[:], compare_op=ALU.not_equal, fill=1.0, base=0,
                                    pattern=[[-1, P]], channel_multiplier=1).then_inc(const_ready, 1)
            link(nc.gpsimd.memset(V1[:], 0.0))
            nc.gpsimd.memset(V1[:, :, :, HD:HD + 1], 1.0).then_inc(const_ready, 1)
            pool.wait_ge(ld_ctx, 32)
            link(nc.gpsimd.tensor_copy(c_parts[:, 0], cT))
            link(nc.gpsimd.tensor_tensor(cT, cT, c_parts[:, 0], ALU.subtract))
            link(nc.gpsimd.tensor_copy(c_parts[:, 1], cT))
            nc.gpsimd.tensor_tensor(c_parts[:, 2], cT, c_parts[:, 1], ALU.subtract).then_inc(c_split, 1)
            pool.wait_ge(dk_written, 16)
            link(nc.gpsimd.memset(V2[:], 0.0))
            link(nc.gpsimd.memset(V2[:, :, :, HD:HD + 1], 1.0))
            nc.gpsimd.tensor_copy(V2[:, :, :, 0:HD], cN.rearrange("p (t g d) -> p t g d", g=G, d=HD)).then_inc(v2_ready, 1)

            def shift(u):
                keys = key_tiles(u) * P
                for i in range(R * QT):
                    pool.wait_ge(sm_ready, R * QT * u + i + 1)
                    n = row_block(u, i) if layer(u) else i
                    row = SM[:, u % SM_RING, n, 0:keys]
                    nc.gpsimd.tensor_scalar(row, row, -1.0, mx[:, u % SM_RING, n:n + 1], ALU.mult, ALU.add).then_inc(sub_done, 1)

            for u in range(UNITS):
                shift(u)
                if u == 0:
                    pool.wait_ge(signs, 3)
                    pool.wait_ge(scales, 4)
                    for i in range(DT):
                        nc.gpsimd.tensor_tensor(woT[:, i, :], woT[:, i, :], so, ALU.mult).then_inc(wo_scaled, 1)

        @block.scalar
        def _(act):
            own = [0]

            def link(ins):
                own[0] += 1
                ins.then_inc(act_own, 1)
                act.wait_ge(act_own, own[0])

            dma_tile(act, planes[:], qweight[:, :, 0:PLANES, :], ld_planes)
            dma_tile(act, scl[:], scales_in, ld_scales)
            dma_tile(act, vo_scales[:, 0:KV], v_scale.rearrange("(a o) -> a o", a=1).broadcast_to([P, KV]), ld_scales)
            dma_tile(act, vo_scales[:, KV:KV + D], o_scale.rearrange("(a o) -> a o", a=1).broadcast_to([P, D]), ld_scales)
            act.wait_ge(ld_wkv, 16)
            nc.scalar.activation(wkvT[:], wkv_raw, ACT.Sign).then_inc(signs, 1)
            act.wait_ge(ld_wq, 16)
            nc.scalar.activation(wqT[:], wq_raw, ACT.Sign).then_inc(signs, 1)
            act.wait_ge(scales, 1)
            act.wait_ge(q_ready, 1)
            nc.scalar.activation(kf, PA[:, 0, :], ACT.Copy, scale=wsum[:, 4:5]).then_inc(q_out, 1)
            act.wait_ge(scales, 2)
            for b in range(B):
                for o in range(DT):
                    act.wait_ge(q_ready, 2 + b * (DT + 1) + (o | 1))
                    nc.scalar.activation(qf[b][:, o], q_psum(b, o), ACT.Copy,
                                         scale=wsum[:, o:o + 1]).then_inc(q_out, 1)
            act.wait_ge(ld_wo, 16)
            nc.scalar.activation(woT[:], wo_raw, ACT.Sign).then_inc(signs, 1)

            def exps(u, k):
                c = first_chunk(u) + k
                if c >= PT_RING:
                    act.wait_ge(pv_done, c - PT_RING + 1)
                else:
                    act.wait_ge(dq_written, Q_WRITES[Q_FIRST - 1])
                for j in range(2):
                    act.wait_ge(t_full, 2 * c + j + 1)
                    nc.scalar.activation(PTs[:, c % PT_RING, j * 512:(j + 1) * 512], PT[:, (2 * c + j) % T_RING, :],
                                         ACT.Exp, scale=-1.0).then_inc(exp_done, 1)

            def unload(u):
                act.wait_ge(pv_done, first_chunk(u + 1))
                if u >= 1:
                    act.wait_ge(pm_full, u)
                nc.scalar.activation(OT, PO[:, 0:S], ACT.Copy).then_inc(po_free, 1)

            def side(what, t):
                if what not in ("turn_o", "turn_x1", "turn_x2", "turn_w"):
                    return
                act.wait_ge(ps_full, PS_USE[(what, t)] + 1)
                turned = PS[:].rearrange("p (o n) -> p o n", o=DT)
                if what in ("turn_o", "turn_x2"):
                    nc.scalar.activation(oT2[t % 2], turned, ACT.Copy).then_inc(ps_free, 1)
                if what == "turn_x1":
                    if t >= 2:
                        act.wait_ge(x1_split, t - 1)
                    nc.scalar.activation(xq[:, t % 2], turned, ACT.Copy, scale=HD ** -0.5).then_inc(ps_free, 1)
                if what == "turn_w":
                    nc.scalar.activation(w_lowT[:, :, t * P:(t + 1) * P], turned, ACT.Copy).then_inc(ps_free, 1)

            def fill(o, n, where, merges_before):
                if where < 0 and o == 0:
                    act.wait_ge(ld_lut, 32)
                    act.wait_ge(q_ready, 2 + B * DT)
                if merges_before:
                    act.wait_ge(merged, merges_before)
                nc.scalar.activation(place(where, o), lut[:, o, 2 * n:2 * n + 1].broadcast_to([P, D]), ACT.Copy).then_inc(leaf_filled, 1)

            oT2 = (oT[:], x2T)
            fills_left = iter(FILLS_LOW)
            for u in range(UNITS):
                for k in range(key_tiles(u)):
                    exps(u, k)
                    if k == 0 and u >= 1:
                        unload(u - 1)
                    for what, t in SIDE[first_chunk(u) + k]:
                        side(what, t)
                    for _ in range(FILL_PACE[first_chunk(u) + k]):
                        fill(*next(fills_left))
            unload(UNITS - 1)
            for what, t in SIDE[first_chunk(UNITS)]:
                side(what, t)

        @block.vector
        def _(dve):
            own = [0]

            def link(ins):
                own[0] += 1
                ins.then_inc(dve_own, 1)
                dve.wait_ge(dve_own, own[0])

            vec = nc.vector
            dve.wait_ge(ld_wkv, 16)
            vec.tensor_reduce(abs_kv, wkv_raw.rearrange("p i o -> p o i"), AX.X, ALU.add,
                              apply_absolute_value=True).then_inc(abs_ready, 1)
            dve.wait_ge(ld_wq, 16)
            vec.tensor_reduce(abs_q, wq_raw.rearrange("p i o -> p o i"), AX.X, ALU.add,
                              apply_absolute_value=True).then_inc(abs_ready, 1)

            def scale(total, given, extra, out_):
                link(vec.tensor_scalar(out_, total, 1.0 / D, 1e-8, ALU.mult, ALU.max))
                return vec.scalar_tensor_tensor(out=out_, in0=out_, scalar=extra, in1=given, op0=ALU.mult, op1=ALU.mult)

            dve.wait_ge(ld_scales, 16 * 3)
            dve.wait_ge(sums_ready, 1)
            scale(PM[:, DT:DT + 1], scl[:, 4:5], 1.0, wsum[:, 4:5]).then_inc(scales, 1)
            dve.wait_ge(sums_ready, 2)
            scale(PM[:, 0:DT], scl[:, 0:4], HD ** -0.5, wsum[:, 0:4]).then_inc(scales, 1)
            def split(src, dst, done):
                yield link(vec.tensor_copy(dst[0], src))
                yield link(vec.tensor_tensor(src, src, dst[0], ALU.subtract))
                yield link(vec.tensor_copy(dst[1], src))
                yield vec.tensor_tensor(dst[2], src, dst[1], ALU.subtract).then_inc(done, 1)

            def finish(steps):
                for _ in steps:
                    pass

            def split_q(n):
                b, o0, o1 = Q_SENDS[n]
                dve.wait_ge(q_out, 1 + b * DT + o1)
                return split(qf[b][:, o0:o1], [q_parts[b][:, s, o0:o1] for s in range(3)], q_split)

            dve.wait_ge(q_out, 1)
            finish(split(kf, [k_parts[:, s] for s in range(3)], q_split))
            for n in range(Q_FIRST):
                finish(split_q(n))
            link(scale(PM[:, P:P + KV], vo_scales[:, 0:KV], 1.0, sv))
            dve.wait_ge(const_ready, 2)
            dve.wait_ge(q_ready, 2 + DT)
            for t in range(NT):
                vec.tensor_tensor(V1[:, t, :, 0:HD], PA[:, 1, t * KV:(t + 1) * KV].rearrange("p (g d) -> p g d", g=G),
                                  sv.rearrange("p (g d) -> p g d", g=G), ALU.mult).then_inc(v_out, 1)

            def output_scales():
                dve.wait_ge(ld_wo, 16)
                vec.tensor_reduce(abs_o, wo_raw.rearrange("p i (a o) -> p a o i", o=S), AX.X, ALU.add,
                                  apply_absolute_value=True).then_inc(abs_ready, 1)
                dve.wait_ge(sums_ready, 3)
                scale(PO[:], vo_scales[:, KV:KV + D], 1.0, so).then_inc(scales, 2)

            def weights():
                for n in range(Q_FIRST, len(Q_SENDS)):
                    yield from split_q(n)
                dve.wait_ge(ld_planes, 16)
                for b in range(8):
                    ins = vec.tensor_scalar(masks[:, :, :, :, b], planes[:], b, 0x01010101,
                                            ALU.logical_shift_right, ALU.bitwise_and)
                yield link(ins)
                leaves = 0
                for kind, o, n, into, *source in STEPS_LOW:
                    if kind == "leaf":
                        leaves += 1
                        dve.wait_ge(leaf_filled, leaves)
                        ins = vec.copy_predicated(inputs(place(into, o)), bit[:, o, 0], inputs(lut[:, o, 2 * n + 1:2 * n + 2].broadcast_to([P, D])))
                        yield link(ins)
                    else:
                        vec.copy_predicated(inputs(place(into, o)), bit[:, o, n], inputs(place(source[0], o))).then_inc(merged, 1)
                        merges[0] += 1
                        dve.wait_ge(merged, merges[0])
                        yield

            merges = [0]

            def maxima(u, i):
                f = first_fill(u) + i
                dve.wait_ge(a_full, f + 1)
                if u >= SM_RING:
                    dve.wait_ge(t_full, 2 * first_chunk(u - SM_RING + 1))
                if layer(u):
                    if u == B * G and i == 0:
                        dve.wait_ge(ld_mask, 16)
                    n = row_block(u, i)
                    vec.tensor_tensor_reduce(SM[:, u % SM_RING, n, :], PA[:, f % 2, :], maskq[:, n % QT, :], 1.0, LOWEST,
                                             ALU.add, ALU.max, mx[:, u % SM_RING, n:n + 1]).then_inc(sm_ready, 1)
                else:
                    for q in range(QT):
                        vec.tensor_scalar(SM[:, u % SM_RING, QT * i + q, 0:S], PA[:, f % 2, q * S:(q + 1) * S], 1.0, None,
                                          ALU.mult, ALU.max, accum_out=mx[:, u % SM_RING, QT * i + q:QT * i + q + 1]).then_inc(sm_ready, 1)

            def normalise(u):
                if u == 0:
                    dve.wait_ge(dc_written, 16)
                dve.wait_ge(pm_full, u + 1)
                pm = PM[:, 0:QT * P].rearrange("p (q r v) -> p q r v", q=QT, r=R)
                link(vec.reciprocal(rsum[:], pm[:, :, :, HD:HD + 1]))
                t = batch(u) * QT
                for q in range(QT):
                    ins = vec.tensor_tensor(
                        O[:, t + q, group(u) * R * HD:(group(u) + 1) * R * HD].rearrange("p (r d) -> p r d", r=R),
                        pm[:, q, :, 0:HD], rsum[:, q].broadcast_to([P, R, HD]), ALU.mult)
                ins.then_inc(pm_free, 1)

            def layernorm(src, dst, ready, t):
                yield link(vec.bn_stats(stats[:], src))
                link(vec.bn_aggr(mv[:], stats[:]))
                link(vec.tensor_scalar(var[:], mv[:, 1:2], EPS, None, ALU.add))
                link(vec.tensor_scalar(root[:, 3:4].bitcast(I32), var[:].bitcast(I32), 1, None, ALU.logical_shift_right))
                yield link(vec.tensor_scalar(root[:, 0:1].bitcast(I32), root[:, 3:4].bitcast(I32), -1.0, float(0x5F3759DF),
                                             ALU.mult, ALU.add))
                for _ in range(3):
                    link(vec.scalar_tensor_tensor(out=root[:, 1:2], in0=root[:, 0:1], scalar=var[:], in1=root[:, 0:1],
                                                  op0=ALU.mult, op1=ALU.mult))
                    link(vec.tensor_scalar(root[:, 2:3], root[:, 1:2], -0.5, 1.5, ALU.mult, ALU.add))
                    link(vec.tensor_tensor(root[:, 0:1], root[:, 0:1], root[:, 2:3], ALU.mult))
                yield
                vec.tensor_scalar(dst, src, mv[:, 0:1], root[:, 0:1], ALU.subtract, ALU.mult).then_inc(ready, 1)
                dve.wait_ge(ready, t + 1)
                yield

            def side(what, t):
                if what == "project_o":
                    if t == 0:
                        dve.wait_ge(ld_xn, 16)
                    dve.wait_ge(ps_full, PS_USE[(what, t)] + 1)
                    vec.tensor_tensor(tmp[:], PS[:], x[:, t], ALU.add).then_inc(ps_free, 1)
                    dve.wait_ge(ps_free, PS_USE[(what, t)] + 1)
                    yield
                    yield from layernorm(tmp[:], x[:, t], x1_ready, t)
                if what == "turn_x1":
                    dve.wait_ge(ps_free, PS_USE[(what, t)] + 1)
                    if t > 0:
                        dve.wait_ge(parts_sent, 16 * t)
                    src = xq[:, t % 2]
                    link(vec.tensor_copy(parts[:, 0], src))
                    yield link(vec.tensor_tensor(src, src, parts[:, 0], ALU.subtract))
                    link(vec.tensor_copy(parts[:, 1], src))
                    yield vec.tensor_tensor(parts[:, 2], src, parts[:, 1], ALU.subtract).then_inc(x1_split, 1)
                if what == "norm_x2":
                    dve.wait_ge(pm_free, B * G + (t // QT + 1) * G)
                    yield link(vec.tensor_tensor(tmp[:], O[:, t], x[:, t], ALU.add))
                    yield from layernorm(tmp[:], x[:, t], x2_ready, t)
                if what == "ffn":
                    dve.wait_ge(x2_ready, t + 1)
                    yield link(vec.tensor_tensor(tmp[:], x[:, t], biasb[:], ALU.add))
                    dve.wait_ge(ps_full, PS_USE[(what, t)] + 1)
                    vec.tensor_tensor(tmp[:], tmp[:], PS[:], ALU.add).then_inc(ps_free, 1)
                    dve.wait_ge(ps_free, PS_USE[(what, t)] + 1)
                    yield
                    yield from layernorm(tmp[:], O[:, t], y_ready, t)

            def between():
                for c in sorted(SIDE):
                    for what, t in SIDE[c]:
                        while now[0] < c + (what != "norm_x2" and c < first_chunk(UNITS)):
                            yield "early"
                        yield from side(what, t)

            work = weights()
            now = [-1]
            rest = between()
            dve.wait_ge(signs, 2)
            for i in range(fills(0)):
                maxima(0, i)
            output_scales()
            dve.wait_ge(signs, 3)
            dve.wait_ge(c_split, 1)
            dve.wait_ge(v2_ready, 1)
            for i in range(fills(1)):
                maxima(1, i)
            for u in range(UNITS):
                ahead = fills(u + 2) if u + 2 < UNITS else 0
                for k in range(key_tiles(u)):
                    for i in range(k * ahead // key_tiles(u), (k + 1) * ahead // key_tiles(u)):
                        maxima(u + 2, i)
                    now[0] = first_chunk(u) + k
                    if k == key_tiles(u) - 1 - layer(u) and u >= 1:
                        normalise(u - 1)
                    steps = 0
                    while steps < STEPS[layer(u)] and next(rest, "early") != "early":
                        steps += 1
                    for _ in range(PACE[first_chunk(u) + k]):
                        next(work, None)
            normalise(UNITS - 1)
            now[0] = first_chunk(UNITS)
            for _ in rest:
                pass

        @block.tensor
        def _(pe):
            mm = nc.tensor.matmul
            def sums(cols, total, n, ready):
                pe.wait_ge(abs_ready, ready)
                if n == 1:
                    last = mm(cols, total, ones[:, 0:1], start=True, stop=True)
                else:
                    last = mm(cols, ones[:], total, start=True, stop=True)
                return last

            pe.wait_ge(const_ready, 1)
            pe.wait_ge(ld_x, 16)
            pe.wait_ge(signs, 1)
            for i in range(DT):
                last = mm(PA[:, 0, :], wkvT[:, i, 0:KV], xT[:, i, :], start=(i == 0), stop=(i == DT - 1))
            last.then_inc(q_ready, 1)
            sums(PM[:, DT:DT + 1], abs_kv[:, 0:KV], 1, 1)
            sums(PM[:, P:P + KV], abs_kv[:, KV:2 * KV], KV, 1).then_inc(sums_ready, 1)
            pe.wait_ge(scales, 1)
            for o in range(DT):
                last = sums(PM[:, o:o + 1], abs_q[:, o * P:(o + 1) * P], 1, 2)
            last.then_inc(sums_ready, 1)
            pe.wait_ge(signs, 2)

            def project_q(b, tiles):
                for o in tiles:
                    for i in range(DT):
                        last = mm(q_psum(b, o), wqT[:, i, o * P:(o + 1) * P], xT[:, i, b * S:(b + 1) * S],
                                  start=(i == 0), stop=(i == DT - 1))
                    last.then_inc(q_ready, 1)

            project_q(0, range(DT))
            for t in range(NT):
                for i in range(DT):
                    last = mm(PA[:, 1, t * KV:(t + 1) * KV], xT[:, i, t * P:(t + 1) * P], wkvT[:, i, KV:2 * KV],
                              start=(i == 0), stop=(i == DT - 1))
            last.then_inc(q_ready, 1)
            project_q(1, range(2))

            def scores(u, i):
                f = first_fill(u) + i
                b, g = batch(u), group(u)
                if i == 0:
                    if layer(u):
                        pe.wait_ge(ka2_ready, 16 * SLOTS)
                        pe.wait_ge(qa2_ready, 16 * SLOTS * (QT * b + 1))
                    else:
                        pe.wait_ge(ka1_ready, 16 * SLOTS)
                        sends = [n for n, (sb_, o0, o1) in enumerate(Q_SENDS) if sb_ == b and o0 <= g * R * HD // P < o1]
                        pe.wait_ge(qa_ready, 16 * SLOTS * (sends[0] + 1))
                if layer(u) and i == R:
                    pe.wait_ge(qa2_ready, 16 * SLOTS * QT * (b + 1))
                if f >= 2:
                    pe.wait_ge(sm_ready, scored(f - 2))
                elif f == 0:
                    pe.wait_ge(q_out, 1)
                else:
                    pe.wait_ge(v_out, NT)
                if layer(u):
                    h, q = g * R + row_block(u, i) // QT, row_block(u, i) % QT
                    last = mm(PA[:, f % 2, :], QA[0:KR, h, b * S + q * P:b * S + (q + 1) * P], KA2[0:KR, g, b * T2:(b + 1) * T2], start=True, stop=True)
                else:
                    for q in range(QT):
                        last = mm(PA[:, f % 2, q * S:(q + 1) * S], QA[0:KR, g * R + i, b * S + q * P:b * S + (q + 1) * P],
                                  KA1[0:KR, g, b * S:(b + 1) * S], start=True, stop=True)
                last.then_inc(a_full, 1)

            def scored(f):
                n = first_fill(B * G)
                return QT * (f + 1) if f < n else QT * n + f + 1 - n

            def turn(u, k, j):
                c = first_chunk(u) + k
                n = 2 * c + j
                if n < T_RING:
                    pe.wait_ge(q_out, 1 + B * DT)
                else:
                    pe.wait_ge(exp_done, n - T_RING + 1)
                for i in range(4 * j, 4 * j + 4):
                    if k == 0:
                        pe.wait_ge(sub_done, R * QT * u + (i // QT + (i % QT) * R if layer(u) else i) + 1)
                    last = nc.tensor.transpose(PT[:, n % T_RING, (i % 4) * P:(i % 4 + 1) * P],
                                               SM[:, u % SM_RING, i, k * P:(k + 1) * P], ident[:])
                last.then_inc(t_full, 1)

            def product(u, k):
                c = first_chunk(u) + k
                pe.wait_ge(exp_done, 2 * c + 2)
                if k == 0 and u == 0:
                    pe.wait_ge(scales, 4)
                if k == 0 and u >= 1:
                    pe.wait_ge(po_free, u)
                V = V2 if layer(u) else V1
                if u == B * G and k == 0:
                    pe.wait_ge(v2_ready, 1)
                for r in range(R):
                    last = mm(PO[VW * r:VW * (r + 1), 0:S], V[:, batch(u) * key_tiles(u) + k, group(u), :],
                              PTs[:, c % PT_RING, r * S:(r + 1) * S], start=(k == 0), stop=(k == key_tiles(u) - 1),
                              tile_position=(0, VW * r))
                last.then_inc(pv_done, 1)

            def ps_claim(n):
                if n == 0:
                    pe.wait_ge(q_out, 1 + B * DT)
                else:
                    pe.wait_ge(ps_free, n)

            def turn_unit(u):
                pe.wait_ge(po_free, u + 1)
                if u == 0:
                    pe.wait_ge(scales, 4)
                else:
                    pe.wait_ge(pm_free, u)
                for q in range(QT):
                    last = nc.tensor.transpose(PM[:, q * P:(q + 1) * P], OT[:, q * P:(q + 1) * P], ident[:])
                last.then_inc(pm_full, 1)

            def side(what, t):
                if what == "norm_x2":
                    return
                n = PS_USE[(what, t)]
                tile = oT if t % 2 == 0 else x2T
                if what == "turn_o":
                    pe.wait_ge(pm_free, (t // QT + 1) * G)
                if what == "turn_x1":
                    pe.wait_ge(x1_ready, t + 1)
                if what == "turn_x2":
                    pe.wait_ge(x2_ready, t + 1)
                if what == "turn_w":
                    pe.wait_ge(merged, (LUT // 2 - 1) * DT)
                ps_claim(n)
                if what == "project_o":
                    pe.wait_ge(wo_scaled, DT)
                    pe.wait_ge(ps_free, PS_USE[("turn_o", t)] + 1)
                    for i in range(DT):
                        last = mm(PS[:], tile[:, i, :], woT[:, i, :], start=(i == 0), stop=(i == DT - 1))
                elif what == "ffn":
                    pe.wait_ge(ps_free, max(PS_USE[("turn_x2", t)], PS_USE[("turn_w", DT - 1)]) + 1)
                    for i in range(DT):
                        last = mm(PS[:], tile[:, i, :], w_lowT[:, i, :], start=(i == 0), stop=(i == DT - 1))
                else:
                    src = {"turn_o": O, "turn_x1": x, "turn_x2": x, "turn_w": w_low}[what]
                    for i in range(DT):
                        last = nc.tensor.transpose(PS[:, i * P:(i + 1) * P], src[:, t, i * P:(i + 1) * P], ident[:])
                last.then_inc(ps_full, 1)

            for i in range(fills(0)):
                scores(0, i)
            project_q(1, range(2, DT))
            sums(PO[:], abs_o, D, 3).then_inc(sums_ready, 1)
            for i in range(fills(1)):
                scores(1, i)
            for u in range(UNITS):
                ahead = fills(u + 2) if u + 2 < UNITS else 0
                for k in range(key_tiles(u)):
                    due = list(range(k * ahead // key_tiles(u), (k + 1) * ahead // key_tiles(u)))
                    for j in range(2):
                        turn(u, k, j)
                        for i in due[j * len(due) // 2:(j + 1) * len(due) // 2]:
                            scores(u + 2, i)
                    if k >= 1:
                        product(u, k - 1)
                    elif u >= 1:
                        product(u - 1, key_tiles(u - 1) - 1)
                    if k == 1 and u >= 1:
                        turn_unit(u - 1)
                    for what, t in SIDE[first_chunk(u) + k]:
                        side(what, t)
            product(UNITS - 1, key_tiles(UNITS - 1) - 1)
            turn_unit(UNITS - 1)
            for what, t in SIDE[first_chunk(UNITS)]:
                side(what, t)


_OUT = ((B, S, D), "float32")


def kernel(**inputs):
    import numpy as np
    import concourse.bacc as bacc
    from concourse.bass_utils import run_bass_kernel_spmd

    a = {k: np.asarray(v) for k, v in inputs.items()}
    x = a["x"].reshape(N, D)
    wk, wv = a["L0_attn_k_weight"], a["L0_attn_v_weight"]
    wkv = np.concatenate([wk, wv], axis=0)
    ctx = a["ctx_1024"].reshape(B * T2, KV)
    lay = {
        "x_tok": x, "x_T": x.T, "wq_T": a["L0_attn_q_weight"].T, "wkv_T": wkv.T, "wo_T": a["L0_attn_o_weight"].T,
        "scales": np.concatenate([a[f"L0_attn_{n}_scale"].reshape(-1, P).T for n in "qk"], axis=1),
        "v_scale": a["L0_attn_v_scale"], "o_scale": a["L0_attn_o_scale"],
                "ctx": ctx, "ctx_T": ctx.T, "mask": a["mask_SxS2_ff0"],
        "qweight": a["L0_ffn_qweight"].reshape(8, DT, P, WORDS).transpose(2, 1, 0, 3),
        "lut4": a["L0_ffn_lut4"].reshape(DT, P, LUT).transpose(1, 0, 2), "lut8": a["L0_ffn_lut8"], "bias": a["L0_ffn_bias"],
    }
    nc = bacc.Bacc("TRN2", target_bir_lowering=False, num_devices=1)
    arrays, args = {}, []
    for name, v in lay.items():
        v = np.ascontiguousarray(v)
        arrays[f"in_{name}"] = v
        args.append(nc.dram_tensor(f"in_{name}", v.shape, mybir.dt.from_np(v.dtype), kind="ExternalInput").ap())
    out = nc.dram_tensor("out_0", (N, D), F32, kind="ExternalOutput").ap()
    kernel_body(nc, *args, out)
    r = run_bass_kernel_spmd(nc, [arrays], core_ids=[0])
    return r.results[0]["out_0"].reshape(B, S, D)
```

```python
from contextlib import ExitStack

import concourse.bass as bass
from concourse import mybir

F32 = mybir.dt.float32
BF16 = mybir.dt.bfloat16
I32 = mybir.dt.int32
U8 = mybir.dt.uint8
ALU = mybir.AluOpType
ACT = mybir.ActivationFunctionType
AX = mybir.AxisListType

P = 128
B, S, D = 2, 256, 512
T2 = 512
H, G, HD = 32, 8, 16
R = H // G
N = B * S
NT = N // P
DT = D // P
QT = S // P
KV = G * HD
VW = 32
Q_PART = (0, 0, 1, 1, 0, 2)
K_PART = (0, 1, 0, 1, 2, 0)
SLOTS = len(Q_PART)
KR = SLOTS * HD
EPS = 1e-5
LOWEST = -3.4e38
HUGE = 1e6
SAFE = 1e30
LUT = 16
PLANES = 4
Q_STEPS = 5
LAG = {"norm_x2": 0, "project_o": 1, "ffn": 1, "turn_x1": 1, "turn_o": 0, "turn_x2": 0, "turn_w": 0}
WARM = (28, 28)
AHEAD = 5
LEAVES = 6
BITS = 32
WORDS = D // BITS
NORM2 = 64.0 * 64.0

STEPS = (4, 2)

SPREAD = (((0, 2), (4, 6)), ((0, 6), (7, 14)))
UNITS = 2 * B * G
SM_RING = 3
PT_RING = 3
T_RING = 3
Q_SENDS = ((0, 0, 1), (0, 1, 2), (0, 2, 4), (1, 0, 4))
Q_WRITES = (16, 32, 64, 80)
Q_FIRST = 3


def layer(u):
    return u // (B * G)


def batch(u):
    return u // G % B


def group(u):
    return u % G


def key_tiles(u):
    return (T2 if layer(u) else S) // P


def first_chunk(u):
    return sum(key_tiles(v) for v in range(u))


def fills(u):
    return R * QT if layer(u) else R


def row_block(u, i):
    return i % R * QT + i // R


def first_fill(u):
    return sum(fills(v) for v in range(u))


def table_plan():
    steps, fills_, free_at, merges = [], [], [(i, 0) for i in range(LEAVES)], 0
    for o in range(DT):
        held = []
        for n in range(LUT // 2):
            place, after = (-1, 0) if n == 0 else free_at.pop(0)
            fills_.append((o, n, place, after))
            steps.append(("leaf", o, n, place))
            held.append((0, place))
            while len(held) > 1 and held[-1][0] == held[-2][0]:
                level, source = held.pop()
                into = held.pop()[1]
                merges += 1
                steps.append(("merge", o, level + 1, into, source))
                free_at.append((source, merges))
                held.append((level + 1, into))
    return steps, fills_


def table_pace():
    steps, _ = table_plan()
    pace, left = {}, Q_STEPS + len(steps)
    for u in range(UNITS):
        for k in range(key_tiles(u)):
            busy = u in (G + 1, G + 2) and k == 0 or layer(u) and k == 3
            pace[first_chunk(u) + k] = n = min(left, 0 if busy else 1)
            left -= n
    assert left == 0
    fill_pace, done, n = {}, -Q_STEPS, 0
    kinds = [s[0] for s in steps]
    for c in sorted(pace):
        done += pace[c]
        due = sum(k == "leaf" for k in kinds[:max(done + AHEAD, 0)])
        fill_pace[c] = due - n
        n = due
    return pace, fill_pace


def kernel_body(nc, x_tok, x_T, wq_T, wkv_T, wo_T, scales_in, v_scale, o_scale,
                ctx, ctx_T, mask, qweight, lut4, lut8, bias, out):
    SIDE = {c: [] for c in range(first_chunk(UNITS) + 1)}
    def side_at(c, what, t):
        SIDE[c].append((what, t))

    for b in range(B):
        for n, t in enumerate(range(b * QT, (b + 1) * QT)):
            at = first_chunk(G * (b + 1) + 1)
            side_at(at + SPREAD[b][0][n], "turn_o", t)
            side_at(at + SPREAD[b][0][n] + 1, "project_o", t)
            side_at(at + SPREAD[b][1][n], "turn_x1", t)
            at = first_chunk(B * G + G * (b + 1) + 1) if b < B - 1 else first_chunk(UNITS)
            late = b < B - 1
            side_at(at, "norm_x2", t)
            side_at(at + (6 + 4 * n) * late, "turn_x2", t)
            side_at(at + (4 * 4 + 2 * n) * late, "ffn", t)
    SIDE[first_chunk(UNITS)].sort(key=lambda s: ("norm_x2", "turn_x2", "ffn").index(s[0]))
    for o in range(DT):
        side_at(first_chunk(3 * G + 4) + o, "turn_w", o)
    STEPS_LOW, FILLS_LOW = table_plan()
    PACE, FILL_PACE = table_pace()
    order = [s for c in sorted(SIDE) for s in SIDE[c] if s[0] != "norm_x2"]
    PS_USE = {what: n for n, what in enumerate(order)}

    with ExitStack() as stack:
        def sb(name, shape, dt=F32):
            return stack.enter_context(nc.sbuf_tensor(name, shape, dt))

        def sem(name):
            return stack.enter_context(nc.semaphore(name))

        ident = sb("ident", [P, P])
        ones = sb("ones", [P, P])
        xT = sb("xT", [P, DT, N])
        wqT = sb("wqT", [P, DT, D])
        wkvT = sb("wkvT", [P, DT, 2 * KV])
        woT = sb("woT", [P, DT, D])
        x = sb("x", [P, NT, D])
        O = sb("O", [P, NT, D])
        QA = sb("QA", [P, H, N], BF16)
        KA1 = sb("KA1", [P, G, N], BF16)
        KA2 = sb("KA2", [P, G, B * T2], BF16)
        V1 = sb("V1", [P, NT, G, VW])
        V2 = sb("V2", [P, B * T2 // P, G, VW])
        SM = sb("SM", [P, SM_RING, R * QT, T2])
        PTs = sb("PTs", [P, PT_RING, R * S])
        maskq = sb("maskq", [P, QT, T2])
        mx = sb("mx", [P, SM_RING, R * QT])
        rsum = sb("rsum", [P, QT, R, 1])
        masks = sb("masks", [P, DT, PLANES, WORDS, 8], I32)
        leaf = sb("leaf", [P, LEAVES - DT, D])
        lut = sb("lut", [P, DT, LUT])
        vo_scales = maskq[:].rearrange("p q t -> p (q t)")[:, 0:KV + D]
        planes = sb("planes", [P, DT, PLANES, WORDS], I32)
        scl = sb("scl", [P, DT + 1])
        wsum = sb("wsum", [P, DT + 1])
        biasb = sb("biasb", [P, D])
        oT = sb("oT", [P, DT, P])
        xq = sb("xq", [P, 2, DT, P])
        parts = sb("parts", [P, 3, DT, P], BF16)
        tmp = sb("tmp", [P, D])
        bound = sb("bound", [P, 5])
        fits = sb("fits", [P, 2], I32)
        limit = sb("limit", [P, 4])
        guard_tmp = sb("guard_tmp", [P, 2, P])
        stats = sb("stats", [P, QT, 6])
        mv = sb("mv", [P, QT, 2])
        var = sb("var", [P, QT])
        root = sb("root", [P, 3, QT])
        def free(slot, start, size):
            return SM[:, slot].rearrange("p a t -> p (a t)")[:, start:start + size]

        wq_raw = free(0, 0, DT * D).rearrange("p (i o) -> p i o", i=DT)
        wkv_raw = free(0, DT * D, DT * 2 * KV).rearrange("p (i o) -> p i o", i=DT)
        abs_q = free(0, DT * (D + 2 * KV), D)
        abs_kv = free(0, DT * (D + 2 * KV) + D, 2 * KV)
        wo_raw = free(1, 0, DT * D).rearrange("p (i o) -> p i o", i=DT)
        cT = free(1, DT * D, B * T2)
        cN = free(1, DT * D + B * T2, B * T2)
        qf = (free(2, 0, DT * S).rearrange("p (o n) -> p o n", o=DT), SM[:, 2, DT:2 * DT, S:T2])
        kf = free(2, 2 * T2, N)
        abs_o = SM[:, 0, 0:D // S, S:T2]
        sv = free(2, 3 * T2, KV)
        so = tmp[:]
        B_COL = 8
        pt_flat = PTs[:].rearrange("p a t -> p (a t)").bitcast(BF16)
        q_parts = [flat[:, 0:3 * DT * S].rearrange("p (s o n) -> p s o n", s=3, o=DT)
                   for flat in (pt_flat, x[:].rearrange("p t d -> p (t d)").bitcast(BF16))]
        k_parts = V2[:].rearrange("p a g v -> p (a g v)").bitcast(BF16)[:, 0:3 * N].rearrange("p (s n) -> p s n", s=3)
        c_parts = O[:].rearrange("p a d -> p (a d)").bitcast(BF16)[:, 0:3 * B * T2].rearrange("p (s n) -> p s n", s=3)
        bit = masks[:].rearrange("p o c w b -> p o c (w b)").bitcast(U8).rearrange("p o c (w b k) -> p o c w k b", w=WORDS, k=4)
        OT = wkvT[:, 0, :]
        x2T = wkvT[:, 1:3, :].rearrange("p a (b n) -> p (a b) n", n=P)
        w_low = xT

        def place(n, o):
            return w_low[:, o] if n < 0 else wqT[:, n] if n < DT else leaf[:, n - DT]

        def inputs(row):
            return row.rearrange("p (w k b) -> p w k b", w=WORDS, k=4)

        w_lowT = wqT

        PT = stack.enter_context(nc.psum_tensor("PT", [P, T_RING, 512], F32))
        PA = stack.enter_context(nc.psum_tensor("PA", [P, 2, 512], F32))
        PO = stack.enter_context(nc.psum_tensor("PO", [P, 512], F32))
        PM = stack.enter_context(nc.psum_tensor("PM", [P, 512], F32))
        PS = stack.enter_context(nc.psum_tensor("PS", [P, 512], F32))

        def q_psum(b, o):
            bank = 2 * b + o // 2
            return (PS[:] if bank == 3 else PT[:, bank, :])[:, (o % 2) * S:(o % 2 + 1) * S]

        LAST_BANKS = {("turn_x2", NT - 1): PA[:, 0], ("ffn", NT - 2): PA[:, 1], ("ffn", NT - 1): PT[:, 0]}

        def ps_bank(what, t):
            return LAST_BANKS.get((what, t), PS[:])

        dq1 = nc.dram_tensor("dq1", (B, 3, D, S), BF16, kind="Internal").ap()
        dk1 = nc.dram_tensor("dk1", (3, KV, N), BF16, kind="Internal").ap()
        dk2 = nc.dram_tensor("dk2", (3, KV, B * T2), BF16, kind="Internal").ap()
        dq2 = nc.dram_tensor("dq2", (NT, 3, D, P), BF16, kind="Internal").ap()

        ld_planes = sem("ld_planes")
        ld_x = sem("ld_x")
        ld_wq = sem("ld_wq")
        ld_wkv = sem("ld_wkv")
        ld_scales = sem("ld_scales")
        ld_wo = sem("ld_wo")
        ld_xn = sem("ld_xn")
        ld_ctx = sem("ld_ctx")
        ld_mask = sem("ld_mask")
        ld_lut = sem("ld_lut")
        const_ready = sem("const_ready")
        pool_own = sem("pool_own")
        dve_own = sem("dve_own")
        guarded = sem("guarded")
        act_own = sem("act_own")
        leaf_filled = sem("leaf_filled")
        merged = sem("merged")
        signs = sem("signs")
        abs_ready = sem("abs_ready")
        sums_ready = sem("sums_ready")
        scales = sem("scales")
        wo_scaled = sem("wo_scaled")
        q_ready = sem("q_ready")
        q_out = sem("q_out")
        v_out = sem("v_out")
        q_split = sem("q_split")
        c_split = sem("c_split")
        v2_ready = sem("v2_ready")
        dq_written = sem("dq_written")
        dk_written = sem("dk_written")
        dc_written = sem("dc_written")
        qa_ready = sem("qa_ready")
        ka1_ready = sem("ka1_ready")
        ka2_ready = sem("ka2_ready")
        a_full = sem("a_full")
        sm_ready = sem("sm_ready")
        sub_done = sem("sub_done")
        t_full = sem("t_full")
        exp_done = sem("exp_done")
        pv_done = sem("pv_done")
        po_free = sem("po_free")
        pm_full = sem("pm_full")
        pm_free = sem("pm_free")
        ps_full = sem("ps_full")
        ps_free = sem("ps_free")
        x1_ready = sem("x1_ready")
        x2_ready = sem("x2_ready")
        x1_split = sem("x1_split")
        parts_sent = sem("parts_sent")
        qa2_ready = sem("qa2_ready")
        y_ready = sem("y_ready")
        y_sent = sem("y_sent")

        block = stack.enter_context(nc.Block())

        def dma_tile(eng, dst, src, s):
            eng.dma_start(dst, src).then_inc(s, 16)

        @block.sync
        def _(sp):
            dma_tile(sp, wkv_raw, wkv_T.rearrange("(t p) n -> p t n", p=P), ld_wkv)
            dma_tile(sp, xT[:], x_T.rearrange("(t p) n -> p t n", p=P), ld_x)
            dma_tile(sp, wq_raw, wq_T.rearrange("(t p) n -> p t n", p=P), ld_wq)
            dma_tile(sp, cT, ctx_T, ld_ctx)
            dma_tile(sp, cN.rearrange("p (t d) -> p t d", d=KV), ctx.rearrange("(t p) d -> p t d", p=P), ld_ctx)
            dma_tile(sp, wo_raw, wo_T.rearrange("(t p) n -> p t n", p=P), ld_wo)
            dma_tile(sp, lut[:], lut4, ld_lut)
            dma_tile(sp, biasb[:], bias.rearrange("(a o) -> a o", a=1).broadcast_to([P, D]), ld_lut)
            sp.wait_ge(q_split, 1)
            dma_tile(sp, dk1.rearrange("s p n -> p s n"), k_parts, dk_written)

            def write_q(n):
                b, o0, o1 = Q_SENDS[n]
                sp.wait_ge(q_split, 2 + n)
                if (o0, o1) == (0, DT):
                    dma_tile(sp, dq1[b].rearrange("s (o p) n -> p (s o) n", p=P), q_parts[b].rearrange("p s o n -> p (s o) n"), dq_written)
                else:
                    for o in range(o0, o1):
                        dma_tile(sp, dq1[b, :, o * P:(o + 1) * P].rearrange("s p n -> p s n"), q_parts[b][:, :, o], dq_written)

            def read_q(n):
                b, o0, o1 = Q_SENDS[n]
                feats, heads, toks = slice(o0 * P, o1 * P), slice(o0 * P // HD, o1 * P // HD), slice(b * S, (b + 1) * S)
                sp.wait_ge(dq_written, Q_WRITES[n])
                for s in range(SLOTS):
                    dma_tile(sp, QA[s * HD:(s + 1) * HD, heads, toks],
                             dq1[b, Q_PART[s], feats].rearrange("(h d) n -> d h n", d=HD), qa_ready)

            write_q(0)
            sp.wait_ge(dk_written, 16)
            for s in range(SLOTS):
                dma_tile(sp, KA1[s * HD:(s + 1) * HD, :, :], dk1[K_PART[s]].rearrange("(g d) n -> d g n", d=HD), ka1_ready)
            read_q(0)
            for n in range(1, Q_FIRST):
                write_q(n)
                read_q(n)
            sp.wait_ge(c_split, 1)
            dma_tile(sp, dk2.rearrange("s p n -> p s n"), c_parts, dc_written)
            sp.wait_ge(scales, 4)
            dma_tile(sp, maskq[:], mask.rearrange("(t p) k -> p t k", p=P), ld_mask)
            for n in range(Q_FIRST, len(Q_SENDS)):
                write_q(n)
                read_q(n)
            dma_tile(sp, x[:], x_tok.rearrange("(t p) d -> p t d", p=P), ld_xn)
            sp.wait_ge(dc_written, 16)
            for s in range(SLOTS):
                dma_tile(sp, KA2[s * HD:(s + 1) * HD, :, :], dk2[K_PART[s]].rearrange("(g d) n -> d g n", d=HD), ka2_ready)
            for t in range(NT):
                sp.wait_ge(x1_split, t + 1)
                dma_tile(sp, dq2[t].rearrange("s (o p) n -> p (s o) n", p=P), parts[:].rearrange("p s o n -> p (s o) n"), parts_sent)
                sp.wait_ge(parts_sent, 16 * (t + 1))
                sp.wait_ge(a_full, first_fill(G * (t // QT + 1)))
                for s in range(SLOTS):
                    dma_tile(sp, QA[s * HD:(s + 1) * HD, :, t * P:(t + 1) * P],
                             dq2[t, Q_PART[s]].rearrange("(h d) n -> d h n", d=HD), qa2_ready)
            for t in range(NT):
                sp.wait_ge(y_ready, t + 1)
                dma_tile(sp, out[t * P:(t + 1) * P, :], O[:, t, :], y_sent)
            sp.wait_ge(y_sent, 16 * NT)

        @block.gpsimd
        def _(pool):
            own = [0]

            def link(ins):
                own[0] += 1
                ins.then_inc(pool_own, 1)
                pool.wait_ge(pool_own, own[0])

            nc.gpsimd.memset(ones[:], 1.0)
            link(nc.gpsimd.memset(ident[:], 0.0))
            nc.gpsimd.affine_select(out=ident[:], in_=ident[:], compare_op=ALU.not_equal, fill=1.0, base=0,
                                    pattern=[[-1, P]], channel_multiplier=1).then_inc(const_ready, 1)
            link(nc.gpsimd.memset(V1[:], 0.0))
            nc.gpsimd.memset(V1[:, :, :, HD:HD + 1], 1.0).then_inc(const_ready, 1)
            pool.wait_ge(ld_ctx, 32)
            link(nc.gpsimd.tensor_copy(c_parts[:, 0], cT))
            link(nc.gpsimd.tensor_tensor(cT, cT, c_parts[:, 0], ALU.subtract))
            link(nc.gpsimd.tensor_copy(c_parts[:, 1], cT))
            nc.gpsimd.tensor_tensor(c_parts[:, 2], cT, c_parts[:, 1], ALU.subtract).then_inc(c_split, 1)
            pool.wait_ge(dk_written, 16)
            link(nc.gpsimd.memset(V2[:], 0.0))
            link(nc.gpsimd.memset(V2[:, :, :, HD:HD + 1], 1.0))
            nc.gpsimd.tensor_copy(V2[:, :, :, 0:HD], cN.rearrange("p (t g d) -> p t g d", g=G, d=HD)).then_inc(v2_ready, 1)

            def shift(u):
                keys = key_tiles(u) * P
                for i in range(R * QT):
                    pool.wait_ge(sm_ready, R * QT * u + i + 1)
                    n = row_block(u, i) if layer(u) else i
                    row = SM[:, u % SM_RING, n, 0:keys]
                    nc.gpsimd.tensor_scalar(row, row, -1.0, mx[:, u % SM_RING, n:n + 1], ALU.mult, ALU.add).then_inc(sub_done, 1)

            for u in range(UNITS):
                shift(u)
                if u == 0:
                    pool.wait_ge(signs, 3)
                    pool.wait_ge(scales, 4)
                    for i in range(DT):
                        nc.gpsimd.tensor_tensor(woT[:, i, :], woT[:, i, :], so, ALU.mult).then_inc(wo_scaled, 1)

        @block.scalar
        def _(act):
            own = [0]

            def link(ins):
                own[0] += 1
                ins.then_inc(act_own, 1)
                act.wait_ge(act_own, own[0])

            dma_tile(act, planes[:], qweight[:, :, 0:PLANES, :], ld_planes)
            dma_tile(act, scl[:], scales_in, ld_scales)
            dma_tile(act, vo_scales[:, 0:KV], v_scale.rearrange("(a o) -> a o", a=1).broadcast_to([P, KV]), ld_scales)
            dma_tile(act, vo_scales[:, KV:KV + D], o_scale.rearrange("(a o) -> a o", a=1).broadcast_to([P, D]), ld_scales)
            act.wait_ge(ld_wkv, 16)
            nc.scalar.activation(wkvT[:], wkv_raw, ACT.Sign).then_inc(signs, 1)
            act.wait_ge(ld_wq, 16)
            nc.scalar.activation(wqT[:], wq_raw, ACT.Sign).then_inc(signs, 1)
            act.wait_ge(scales, 1)
            act.wait_ge(q_ready, 1)
            nc.scalar.activation(kf, PA[:, 0, :], ACT.Copy, scale=wsum[:, 4:5]).then_inc(q_out, 1)
            act.wait_ge(scales, 2)
            for b in range(B):
                for o in range(DT):
                    act.wait_ge(q_ready, 2 + b * (DT + 1) + (o | 1))
                    nc.scalar.activation(qf[b][:, o], q_psum(b, o), ACT.Copy,
                                         scale=wsum[:, o:o + 1]).then_inc(q_out, 1)
            act.wait_ge(ld_wo, 16)
            nc.scalar.activation(woT[:], wo_raw, ACT.Sign).then_inc(signs, 1)

            def exps(u, k):
                c = first_chunk(u) + k
                if c >= PT_RING:
                    act.wait_ge(pv_done, c - PT_RING + 1)
                else:
                    act.wait_ge(dq_written, Q_WRITES[Q_FIRST - 1])
                for j in range(2):
                    act.wait_ge(t_full, 2 * c + j + 1)
                    nc.scalar.activation(PTs[:, c % PT_RING, j * 512:(j + 1) * 512], PT[:, (2 * c + j) % T_RING, :],
                                         ACT.Exp, scale=-1.0).then_inc(exp_done, 1)

            def unload(u):
                act.wait_ge(pv_done, first_chunk(u + 1))
                if u >= 1:
                    act.wait_ge(pm_full, u)
                nc.scalar.activation(OT, PO[:, 0:S], ACT.Copy).then_inc(po_free, 1)

            def side(what, t):
                if what not in ("turn_o", "turn_x1", "turn_x2", "turn_w"):
                    return
                act.wait_ge(ps_full, PS_USE[(what, t)] + 1)
                turned = ps_bank(what, t).rearrange("p (o n) -> p o n", o=DT)
                if what in ("turn_o", "turn_x2"):
                    nc.scalar.activation(oT2[t % 2], turned, ACT.Copy).then_inc(ps_free, 1)
                if what == "turn_x1":
                    if t >= 2:
                        act.wait_ge(x1_split, t - 1)
                    nc.scalar.activation(xq[:, t % 2], turned, ACT.Copy, scale=HD ** -0.5).then_inc(ps_free, 1)
                if what == "turn_w":
                    nc.scalar.activation(w_lowT[:, :, t * P:(t + 1) * P], turned, ACT.Copy).then_inc(ps_free, 1)

            def fill(o, n, where, merges_before):
                if where < 0 and o == 0:
                    act.wait_ge(ld_lut, 32)
                    act.wait_ge(q_ready, 2 + B * DT)
                if merges_before:
                    act.wait_ge(merged, merges_before)
                nc.scalar.activation(place(where, o), lut[:, o, 2 * n:2 * n + 1].broadcast_to([P, D]), ACT.Copy).then_inc(leaf_filled, 1)

            oT2 = (oT[:], x2T)
            fills_left = iter(FILLS_LOW)
            for u in range(UNITS):
                for k in range(key_tiles(u)):
                    exps(u, k)
                    if k == 0 and u >= 1:
                        unload(u - 1)
                    for what, t in SIDE[first_chunk(u) + k]:
                        side(what, t)
                    for _ in range(FILL_PACE[first_chunk(u) + k]):
                        fill(*next(fills_left))
            unload(UNITS - 1)
            for what, t in SIDE[first_chunk(UNITS)]:
                side(what, t)

        @block.vector
        def _(dve):
            own = [0]

            def link(ins):
                own[0] += 1
                ins.then_inc(dve_own, 1)
                dve.wait_ge(dve_own, own[0])

            vec = nc.vector
            dve.wait_ge(ld_wkv, 16)
            vec.tensor_reduce(abs_kv, wkv_raw.rearrange("p i o -> p o i"), AX.X, ALU.add,
                              apply_absolute_value=True).then_inc(abs_ready, 1)
            dve.wait_ge(ld_x, 16)
            vec.tensor_reduce(bound[:, 0:1], xT[:].rearrange("p i n -> p (i n)"), AX.X, ALU.max, apply_absolute_value=True)
            dve.wait_ge(abs_ready, 1)
            vec.tensor_reduce(bound[:, 2:3], abs_kv, AX.X, ALU.add)
            dve.wait_ge(ld_wq, 16)
            link(vec.tensor_reduce(abs_q, wq_raw.rearrange("p i o -> p o i"), AX.X, ALU.add, apply_absolute_value=True))
            dve.wait_ge(ld_scales, 16 * 3)
            vec.tensor_reduce(bound[:, 3:4], scl[:], AX.X, ALU.add, apply_absolute_value=True)
            vec.tensor_reduce(bound[:, 1:2], abs_q, AX.X, ALU.add).then_inc(abs_ready, 1)

            def scale(total, given, extra, out_):
                link(vec.tensor_scalar(out_, total, 1.0 / D, 1e-8, ALU.mult, ALU.max))
                return vec.scalar_tensor_tensor(out=out_, in0=out_, scalar=extra, in1=given, op0=ALU.mult, op1=ALU.mult)

            dve.wait_ge(sums_ready, 1)
            scale(PM[:, DT:DT + 1], scl[:, 4:5], 1.0, wsum[:, 4:5]).then_inc(scales, 1)
            dve.wait_ge(sums_ready, 2)
            scale(PM[:, 0:DT], scl[:, 0:4], HD ** -0.5, wsum[:, 0:4]).then_inc(scales, 1)
            def split(src, dst, done):
                yield link(vec.tensor_copy(dst[0], src))
                yield link(vec.tensor_tensor(src, src, dst[0], ALU.subtract))
                yield link(vec.tensor_copy(dst[1], src))
                yield vec.tensor_tensor(dst[2], src, dst[1], ALU.subtract).then_inc(done, 1)

            guards = [0]

            def guard(flag, *rows):
                def step(ins):
                    guards[0] += 1
                    ins.then_inc(guarded, 1)
                    dve.wait_ge(guarded, guards[0])

                before = guards[0]
                with dve.If_eq(flag, 0):
                    low = guard_tmp[:, 0]
                    high = guard_tmp[:, 1]
                    for row in rows:
                        if len(row.shape) == 3:
                            low, high = (guard_tmp[:, i].rearrange("p (g d) -> p g d", g=G) for i in range(2))
                        step(vec.tensor_scalar(high, row, 0.0, HUGE, ALU.max, ALU.min))
                        step(vec.tensor_scalar(low, row, 0.0, -HUGE, ALU.min, ALU.max))
                        step(vec.tensor_tensor(low, low, high, ALU.add))
                        step(vec.tensor_scalar(high, row, 0.0, 0.0, ALU.mult, ALU.is_equal))
                        step(vec.copy_predicated(low, high.bitcast(I32), row))
                        step(vec.tensor_copy(row, low))
                with dve.If_ne(flag, 0):
                    vec.tensor_copy(guard_tmp[0:1, 0, 0:1], ident[0:1, 0:1]).then_inc(guarded, guards[0] - before)
                dve.wait_ge(guarded, guards[0])

            def columns(rows):
                return [rows[:, o, n:n + P] for o in range(rows.shape[1]) for n in range(0, rows.shape[2], P)]

            def finish(steps):
                for _ in steps:
                    pass

            def split_q(n):
                b, o0, o1 = Q_SENDS[n]
                dve.wait_ge(q_out, 1 + b * DT + o1)
                guard(qkv_fits, *columns(qf[b][:, o0:o1]))
                return split(qf[b][:, o0:o1], [q_parts[b][:, s, o0:o1] for s in range(3)], q_split)

            all_x, all_w, all_s, most = (limit[:, i:i + 1] for i in range(4))
            vec.tensor_reduce(all_s, vo_scales[:, 0:KV], AX.X, ALU.add, apply_absolute_value=True)
            vec.tensor_scalar(all_w, PM[:, B_COL + 1:B_COL + 2], 1.0, None, ALU.add)
            link(vec.tensor_scalar(all_x, PM[:, B_COL:B_COL + 1], float(D), None, ALU.mult))
            vec.tensor_tensor(all_w, all_w, PM[:, B_COL + 2:B_COL + 3], ALU.add)
            link(vec.tensor_tensor(all_s, all_s, PM[:, B_COL + 3:B_COL + 4], ALU.add))
            link(vec.tensor_tensor(all_w, all_w, all_s, ALU.mult))
            link(vec.scalar_tensor_tensor(out=most, in0=all_w, scalar=1.0, in1=all_x, op0=ALU.add, op1=ALU.mult))
            link(vec.tensor_scalar(fits[:, 0:1], most, SAFE, None, ALU.is_lt))
            qkv_fits, o_fits = dve.alloc_register("qkv_fits"), dve.alloc_register("o_fits")
            dve.reg_load(qkv_fits, fits[0:1, 0:1])
            dve.wait_ge(const_ready, 1)
            dve.wait_ge(q_out, 1)
            guard(qkv_fits, *columns(kf.rearrange("p (a n) -> p a n", a=1)))
            finish(split(kf, [k_parts[:, s] for s in range(3)], q_split))
            for n in range(Q_FIRST):
                finish(split_q(n))
            link(scale(PM[:, P:P + KV], vo_scales[:, 0:KV], 1.0, sv))
            dve.wait_ge(const_ready, 2)
            dve.wait_ge(q_ready, 2 + DT)
            for t in range(NT):
                vec.tensor_tensor(V1[:, t, :, 0:HD], PA[:, 1, t * KV:(t + 1) * KV].rearrange("p (g d) -> p g d", g=G),
                                  sv.rearrange("p (g d) -> p g d", g=G), ALU.mult).then_inc(v_out, 1)
            dve.wait_ge(v_out, NT)
            guard(qkv_fits, *[V1[:, t, :, 0:HD] for t in range(NT)])

            def output_scales():
                dve.wait_ge(sums_ready, 3)
                link(scale(PO[:], vo_scales[:, KV:KV + D], 1.0, so))
                link(vec.tensor_reduce(all_s, so, AX.X, ALU.add, apply_absolute_value=True))
                link(vec.tensor_scalar(all_s, all_s, 1.0, float(D), ALU.add, ALU.mult))
                link(vec.tensor_tensor(most, most, all_s, ALU.mult))
                vec.tensor_scalar(fits[:, 1:2], most, SAFE, None, ALU.is_lt).then_inc(scales, 2)
                dve.wait_ge(scales, 4)
                dve.reg_load(o_fits, fits[0:1, 1:2])

            def weights():
                for n in range(Q_FIRST, len(Q_SENDS)):
                    yield from split_q(n)
                dve.wait_ge(ld_planes, 16)
                for b in range(8):
                    ins = vec.tensor_scalar(masks[:, :, :, :, b], planes[:], b, 0x01010101,
                                            ALU.logical_shift_right, ALU.bitwise_and)
                yield link(ins)
                leaves = 0
                for kind, o, n, into, *source in STEPS_LOW:
                    if kind == "leaf":
                        leaves += 1
                        dve.wait_ge(leaf_filled, leaves)
                        ins = vec.copy_predicated(inputs(place(into, o)), bit[:, o, 0], inputs(lut[:, o, 2 * n + 1:2 * n + 2].broadcast_to([P, D])))
                        yield link(ins)
                    else:
                        vec.copy_predicated(inputs(place(into, o)), bit[:, o, n], inputs(place(source[0], o))).then_inc(merged, 1)
                        merges[0] += 1
                        dve.wait_ge(merged, merges[0])
                        yield

            merges = [0]

            def maxima(u, i):
                f = first_fill(u) + i
                dve.wait_ge(a_full, f + 1)
                if u >= SM_RING:
                    dve.wait_ge(t_full, 2 * first_chunk(u - SM_RING + 1))
                if layer(u):
                    if u == B * G and i == 0:
                        dve.wait_ge(ld_mask, 16)
                    n = row_block(u, i)
                    vec.tensor_tensor_reduce(SM[:, u % SM_RING, n, :], PA[:, f % 2, :], maskq[:, n % QT, :], 1.0, LOWEST,
                                             ALU.add, ALU.max, mx[:, u % SM_RING, n:n + 1]).then_inc(sm_ready, 1)
                else:
                    for q in range(QT):
                        vec.tensor_scalar(SM[:, u % SM_RING, QT * i + q, 0:S], PA[:, f % 2, q * S:(q + 1) * S], 1.0, None,
                                          ALU.mult, ALU.max, accum_out=mx[:, u % SM_RING, QT * i + q:QT * i + q + 1]).then_inc(sm_ready, 1)

            def normalise(u):
                if u == 0:
                    dve.wait_ge(dc_written, 16)
                dve.wait_ge(pm_full, u + 1)
                pm = PM[:, 0:QT * P].rearrange("p (q r v) -> p q r v", q=QT, r=R)
                link(vec.reciprocal(rsum[:], pm[:, :, :, HD:HD + 1]))
                t = batch(u) * QT
                for q in range(QT):
                    ins = vec.tensor_tensor(
                        O[:, t + q, group(u) * R * HD:(group(u) + 1) * R * HD].rearrange("p (r d) -> p r d", r=R),
                        pm[:, q, :, 0:HD], rsum[:, q].broadcast_to([P, R, HD]), ALU.mult)
                ins.then_inc(pm_free, 1)

            def layernorm(src, dst, ready, t):
                n = len(src)
                for i in range(n):
                    ins = vec.bn_stats(stats[:, i], src[i])
                    if i == n - 1:
                        yield link(ins)
                for i in range(n):
                    ins = vec.bn_aggr(mv[:, i], stats[:, i])
                link(ins)
                v, y, guess, t1 = var[:, 0:n], root[:, 0, 0:n], root[:, 1, 0:n], root[:, 2, 0:n]
                link(vec.tensor_scalar(v, mv[:, 0:n, 1], EPS, None, ALU.add))
                link(vec.tensor_scalar(guess.bitcast(I32), v.bitcast(I32), 1, None, ALU.logical_shift_right))
                yield link(vec.tensor_scalar(y.bitcast(I32), guess.bitcast(I32), -1.0, float(0x5F3759DF), ALU.mult, ALU.add))
                for _ in range(3):
                    link(vec.scalar_tensor_tensor(out=t1, in0=y, scalar=-0.5, in1=y, op0=ALU.mult, op1=ALU.mult))
                    link(vec.tensor_tensor(t1, t1, v, ALU.mult))
                    link(vec.scalar_tensor_tensor(out=y, in0=t1, scalar=1.5, in1=y, op0=ALU.add, op1=ALU.mult))
                yield
                for i in range(n):
                    vec.tensor_scalar(dst[i], src[i], mv[:, i, 0:1], y[:, i:i + 1], ALU.subtract, ALU.mult).then_inc(ready, 1)
                dve.wait_ge(ready, t + n)
                yield

            def side(what, t):
                if what == "project_o":
                    if t == 0:
                        dve.wait_ge(ld_xn, 16)
                    dve.wait_ge(ps_full, PS_USE[(what, t)] + 1)
                    guard(o_fits, *columns(PS[:].rearrange("p (a n) -> p a n", a=1)))
                    vec.tensor_tensor(tmp[:], PS[:], x[:, t], ALU.add).then_inc(ps_free, 1)
                    dve.wait_ge(ps_free, PS_USE[(what, t)] + 1)
                    yield
                    yield from layernorm([tmp[:]], [x[:, t]], x1_ready, t)
                if what == "turn_x1":
                    dve.wait_ge(ps_free, PS_USE[(what, t)] + 1)
                    if t > 0:
                        dve.wait_ge(parts_sent, 16 * t)
                    src = xq[:, t % 2]
                    link(vec.tensor_copy(parts[:, 0], src))
                    yield link(vec.tensor_tensor(src, src, parts[:, 0], ALU.subtract))
                    link(vec.tensor_copy(parts[:, 1], src))
                    yield vec.tensor_tensor(parts[:, 2], src, parts[:, 1], ALU.subtract).then_inc(x1_split, 1)
                if what == "norm_x2":
                    dve.wait_ge(pm_free, B * G + (t // QT + 1) * G)
                    if t < NT - QT:
                        yield link(vec.tensor_tensor(tmp[:], O[:, t], x[:, t], ALU.add))
                        yield from layernorm([tmp[:]], [x[:, t]], x2_ready, t)
                    elif t == NT - QT:
                        sums_ = [tmp[:], xq[:, 0].rearrange("p o n -> p (o n)")]
                        for i in range(QT):
                            ins = vec.tensor_tensor(sums_[i], O[:, t + i], x[:, t + i], ALU.add)
                        yield link(ins)
                        yield from layernorm(sums_, [x[:, t + i] for i in range(QT)], x2_ready, t)
                if what == "ffn":
                    dve.wait_ge(x2_ready, t + 1)
                    yield link(vec.tensor_tensor(tmp[:], x[:, t], biasb[:], ALU.add))
                    dve.wait_ge(ps_full, PS_USE[(what, t)] + 1)
                    vec.tensor_tensor(tmp[:], tmp[:], ps_bank(what, t), ALU.add).then_inc(ps_free, 1)
                    dve.wait_ge(ps_free, PS_USE[(what, t)] + 1)
                    yield
                    yield from layernorm([tmp[:]], [O[:, t]], y_ready, t)

            def between():
                for c in sorted(SIDE):
                    for what, t in SIDE[c]:
                        while now[0] < c + (0 if c == first_chunk(UNITS) else LAG[what]):
                            yield "early"
                        yield from side(what, t)

            work = weights()
            now = [-1]
            rest = between()
            dve.wait_ge(signs, 2)
            dve.wait_ge(ld_wo, 16)
            vec.tensor_reduce(abs_o, wo_raw.rearrange("p i (a o) -> p a o i", o=S), AX.X, ALU.add,
                              apply_absolute_value=True).then_inc(abs_ready, 1)
            for i in range(fills(0)):
                maxima(0, i)
            output_scales()
            dve.wait_ge(signs, 3)
            dve.wait_ge(c_split, 1)
            dve.wait_ge(v2_ready, 1)
            for i in range(fills(1)):
                maxima(1, i)
            for u in range(UNITS):
                ahead = fills(u + 2) if u + 2 < UNITS else 0
                for k in range(key_tiles(u)):
                    for i in range(k * ahead // key_tiles(u), (k + 1) * ahead // key_tiles(u)):
                        maxima(u + 2, i)
                    now[0] = first_chunk(u) + k
                    if k == key_tiles(u) - 1 - layer(u) and u >= 1:
                        normalise(u - 1)
                    steps = 0
                    while steps < STEPS[layer(u)] and next(rest, "early") != "early":
                        steps += 1
                    for _ in range(PACE[first_chunk(u) + k]):
                        next(work, None)
            normalise(UNITS - 1)
            now[0] = first_chunk(UNITS)
            for _ in rest:
                pass

        @block.tensor
        def _(pe):
            mm = nc.tensor.matmul
            def sums(cols, total, n, ready):
                pe.wait_ge(abs_ready, ready)
                if n == 1:
                    last = mm(cols, total, ones[:, 0:1], start=True, stop=True)
                else:
                    last = mm(cols, ones[:], total, start=True, stop=True)
                return last

            pe.wait_ge(const_ready, 1)
            for _ in range(WARM[0]):
                mm(PT[:, 0, 0:P], ones[:], ident[:], start=True, stop=True)
            pe.wait_ge(ld_x, 16)
            pe.wait_ge(signs, 1)
            for i in range(DT):
                last = mm(PA[:, 0, :], wkvT[:, i, 0:KV], xT[:, i, :], start=(i == 0), stop=(i == DT - 1))
            last.then_inc(q_ready, 1)
            sums(PM[:, DT:DT + 1], abs_kv[:, 0:KV], 1, 1)
            sums(PM[:, P:P + KV], abs_kv[:, KV:2 * KV], KV, 1).then_inc(sums_ready, 1)
            def project_q(b, tiles):
                for o in tiles:
                    for i in range(DT):
                        last = mm(q_psum(b, o), wqT[:, i, o * P:(o + 1) * P], xT[:, i, b * S:(b + 1) * S],
                                  start=(i == 0), stop=(i == DT - 1))
                    last.then_inc(q_ready, 1)

            pe.wait_ge(signs, 2)
            project_q(0, range(1))
            pe.wait_ge(scales, 1)
            for o in range(DT):
                last = sums(PM[:, o:o + 1], abs_q[:, o * P:(o + 1) * P], 1, 2)
            mm(PM[:, B_COL:B_COL + 4], ones[:], bound[:, 0:4], start=True, stop=True).then_inc(sums_ready, 1)
            project_q(0, range(1, DT))
            for t in range(NT):
                for i in range(DT):
                    last = mm(PA[:, 1, t * KV:(t + 1) * KV], xT[:, i, t * P:(t + 1) * P], wkvT[:, i, KV:2 * KV],
                              start=(i == 0), stop=(i == DT - 1))
            last.then_inc(q_ready, 1)
            project_q(1, range(DT))
            sums(PO[:], abs_o, D, 3).then_inc(sums_ready, 1)

            def scores(u, i):
                f = first_fill(u) + i
                b, g = batch(u), group(u)
                if i == 0:
                    if layer(u):
                        pe.wait_ge(ka2_ready, 16 * SLOTS)
                        pe.wait_ge(qa2_ready, 16 * SLOTS * (QT * b + 1))
                    else:
                        pe.wait_ge(ka1_ready, 16 * SLOTS)
                        sends = [n for n, (sb_, o0, o1) in enumerate(Q_SENDS) if sb_ == b and o0 <= g * R * HD // P < o1]
                        pe.wait_ge(qa_ready, 16 * SLOTS * (sends[0] + 1))
                if layer(u) and i == R:
                    pe.wait_ge(qa2_ready, 16 * SLOTS * QT * (b + 1))
                if f >= 2:
                    pe.wait_ge(sm_ready, scored(f - 2))
                elif f == 0:
                    pe.wait_ge(q_out, 1)
                else:
                    pe.wait_ge(v_out, NT)
                if layer(u):
                    h, q = g * R + row_block(u, i) // QT, row_block(u, i) % QT
                    last = mm(PA[:, f % 2, :], QA[0:KR, h, b * S + q * P:b * S + (q + 1) * P], KA2[0:KR, g, b * T2:(b + 1) * T2], start=True, stop=True)
                else:
                    for q in range(QT):
                        last = mm(PA[:, f % 2, q * S:(q + 1) * S], QA[0:KR, g * R + i, b * S + q * P:b * S + (q + 1) * P],
                                  KA1[0:KR, g, b * S:(b + 1) * S], start=True, stop=True)
                last.then_inc(a_full, 1)

            def scored(f):
                n = first_fill(B * G)
                return QT * (f + 1) if f < n else QT * n + f + 1 - n

            def turn(u, k, j):
                c = first_chunk(u) + k
                n = 2 * c + j
                if n < T_RING:
                    pe.wait_ge(q_out, 1 + B * DT)
                else:
                    pe.wait_ge(exp_done, n - T_RING + 1)
                for i in range(4 * j, 4 * j + 4):
                    if k == 0:
                        pe.wait_ge(sub_done, R * QT * u + (i // QT + (i % QT) * R if layer(u) else i) + 1)
                    last = nc.tensor.transpose(PT[:, n % T_RING, (i % 4) * P:(i % 4 + 1) * P],
                                               SM[:, u % SM_RING, i, k * P:(k + 1) * P], ident[:])
                last.then_inc(t_full, 1)

            def product(u, k):
                c = first_chunk(u) + k
                pe.wait_ge(exp_done, 2 * c + 2)
                if k == 0 and u == 0:
                    pe.wait_ge(scales, 4)
                if k == 0 and u >= 1:
                    pe.wait_ge(po_free, u)
                V = V2 if layer(u) else V1
                if u == B * G and k == 0:
                    pe.wait_ge(v2_ready, 1)
                for r in range(R):
                    last = mm(PO[VW * r:VW * (r + 1), 0:S], V[:, batch(u) * key_tiles(u) + k, group(u), :],
                              PTs[:, c % PT_RING, r * S:(r + 1) * S], start=(k == 0), stop=(k == key_tiles(u) - 1),
                              tile_position=(0, VW * r))
                last.then_inc(pv_done, 1)

            def warm(bank, times):
                for _ in range(times):
                    mm(bank[:, 0:P], ones[:], ident[:], start=True, stop=True)

            def ps_claim(what, t, n):
                if (what, t) in LAST_BANKS:
                    return
                if n == 0:
                    pe.wait_ge(q_out, 1 + B * DT)
                else:
                    pe.wait_ge(ps_free, n)

            def turn_unit(u):
                pe.wait_ge(po_free, u + 1)
                if u == 0:
                    pe.wait_ge(scales, 4)
                else:
                    pe.wait_ge(pm_free, u)
                for q in range(QT):
                    last = nc.tensor.transpose(PM[:, q * P:(q + 1) * P], OT[:, q * P:(q + 1) * P], ident[:])
                last.then_inc(pm_full, 1)

            def side(what, t):
                if what == "norm_x2":
                    return
                n = PS_USE[(what, t)]
                tile = oT if t % 2 == 0 else x2T
                if what == "turn_o":
                    pe.wait_ge(pm_free, (t // QT + 1) * G)
                if what == "turn_x1":
                    pe.wait_ge(x1_ready, t + 1)
                if what == "turn_x2":
                    pe.wait_ge(x2_ready, t + 1)
                if what == "turn_w":
                    pe.wait_ge(merged, (LUT // 2 - 1) * DT)
                ps_claim(what, t, n)
                bank = ps_bank(what, t)
                if what == "project_o":
                    pe.wait_ge(wo_scaled, DT)
                    pe.wait_ge(ps_free, PS_USE[("turn_o", t)] + 1)
                    for i in range(DT):
                        last = mm(PS[:], tile[:, i, :], woT[:, i, :], start=(i == 0), stop=(i == DT - 1))
                elif what == "ffn":
                    turned = ("turn_x2", t if t < NT - QT else NT - 1)
                    pe.wait_ge(ps_free, max(PS_USE[turned], PS_USE[("turn_w", DT - 1)]) + 1)
                    for i in range(DT):
                        last = mm(bank, tile[:, i, :], w_lowT[:, i, :], start=(i == 0), stop=(i == DT - 1))
                else:
                    src = {"turn_o": O, "turn_x1": x, "turn_x2": x, "turn_w": w_low}[what]
                    for i in range(DT):
                        last = nc.tensor.transpose(bank[:, i * P:(i + 1) * P], src[:, t, i * P:(i + 1) * P], ident[:])
                last.then_inc(ps_full, 1)

            for i in range(fills(0)):
                scores(0, i)
            for i in range(fills(1)):
                scores(1, i)
            for u in range(UNITS):
                ahead = fills(u + 2) if u + 2 < UNITS else 0
                for k in range(key_tiles(u)):
                    due = list(range(k * ahead // key_tiles(u), (k + 1) * ahead // key_tiles(u)))
                    for j in range(2):
                        turn(u, k, j)
                        for i in due[j * len(due) // 2:(j + 1) * len(due) // 2]:
                            scores(u + 2, i)
                    if k >= 1:
                        product(u, k - 1)
                    elif u >= 1:
                        product(u - 1, key_tiles(u - 1) - 1)
                    if k == 1 and u >= 1:
                        turn_unit(u - 1)
                    for what, t in SIDE[first_chunk(u) + k]:
                        side(what, t)
            product(UNITS - 1, key_tiles(UNITS - 1) - 1)
            turn_unit(UNITS - 1)
            pe.wait_ge(exp_done, 2 * first_chunk(UNITS))
            warm(PT[:, 0], WARM[1])
            for what, t in SIDE[first_chunk(UNITS)]:
                side(what, t)


_OUT = ((B, S, D), "float32")


def kernel(**inputs):
    import numpy as np
    import concourse.bacc as bacc
    from concourse.bass_utils import run_bass_kernel_spmd

    a = {k: np.asarray(v) for k, v in inputs.items()}
    x = a["x"].reshape(N, D)
    wk, wv = a["L0_attn_k_weight"], a["L0_attn_v_weight"]
    wkv = np.concatenate([wk, wv], axis=0)
    ctx = a["ctx_1024"].reshape(B * T2, KV)
    lay = {
        "x_tok": x, "x_T": x.T, "wq_T": a["L0_attn_q_weight"].T, "wkv_T": wkv.T, "wo_T": a["L0_attn_o_weight"].T,
        "scales": np.concatenate([a[f"L0_attn_{n}_scale"].reshape(-1, P).T for n in "qk"], axis=1),
        "v_scale": a["L0_attn_v_scale"], "o_scale": a["L0_attn_o_scale"],
                "ctx": ctx, "ctx_T": ctx.T, "mask": a["mask_SxS2_ff0"],
        "qweight": a["L0_ffn_qweight"].reshape(8, DT, P, WORDS).transpose(2, 1, 0, 3),
        "lut4": a["L0_ffn_lut4"].reshape(DT, P, LUT).transpose(1, 0, 2), "lut8": a["L0_ffn_lut8"], "bias": a["L0_ffn_bias"],
    }
    nc = bacc.Bacc("TRN2", target_bir_lowering=False, num_devices=1)
    arrays, args = {}, []
    for name, v in lay.items():
        v = np.ascontiguousarray(v)
        arrays[f"in_{name}"] = v
        args.append(nc.dram_tensor(f"in_{name}", v.shape, mybir.dt.from_np(v.dtype), kind="ExternalInput").ap())
    out = nc.dram_tensor("out_0", (N, D), F32, kind="ExternalOutput").ap()
    kernel_body(nc, *args, out)
    r = run_bass_kernel_spmd(nc, [arrays], core_ids=[0])
    return r.results[0]["out_0"].reshape(B, S, D)
```
